# Optimizing a Trainium2 kernel written in Bass

```python
import numpy as np
import jax
import jax.numpy as jnp

def _softmax(x, axis=-1):
    return jax.nn.softmax(x, axis=axis)

def _gelu(x):
    return jax.nn.gelu(x, approximate=True)

def _silu(x):
    return jax.nn.silu(x)

def _sigmoid(x):
    return jax.nn.sigmoid(x)

def _layernorm(x, axis=-1, eps=1e-05):
    m = jnp.mean(x, axis=axis, keepdims=True)
    v = jnp.var(x, axis=axis, keepdims=True)
    return (x - m) / jnp.sqrt(v + eps)

def _scatter_add(tgt, idx, src, axis=0):
    return tgt.at[idx].add(src)

def _segment_sum(src, seg, n):
    return jax.ops.segment_sum(src, seg, n)
kernel_name = 'mk_prb_d1_jaxref_r4_582514'

def setup_inputs(seed: int=0):
    np.random.seed(seed)
    _w = jnp.asarray

    def _L0_attn_setup():
        import jax, jax.numpy as jnp
        import numpy as np
        HEAD = 64

        def wkv6(r, k, v, w, u):
            B, T, C = r.shape
            N = C // HEAD
            shp = lambda a: a.reshape(B, T, N, HEAD).transpose(1, 0, 2, 3)
            rT, kT, vT = (shp(r), shp(k), shp(v))
            dT = jnp.exp(shp(w))
            uu = u[None]

            def step(S, inp):
                rt, kt, vt, dt = inp
                kv = vt[..., :, None] * kt[..., None, :]
                yt = jnp.einsum('bnj,bnij->bni', rt, S + uu[..., None, :] * kv)
                S = S * dt[..., None, :] + kv
                return (S, yt)
            S0 = jnp.zeros((B, N, HEAD, HEAD), r.dtype)
            _, ys = jax.lax.scan(step, S0, (rT, kT, vT, dT))
            return ys.transpose(1, 0, 2, 3).reshape(B, T, C)
        key = jax.random.key(seed)
        B, T, C = (2, 256, 256)
        N = C // HEAD
        depth, layer_id = (24, 12)
        r01 = layer_id / (depth - 1)
        r1a0 = 1.0 - layer_id / depth
        ddd = np.arange(C, dtype=np.float64) / C
        miu_x = (1.0 - ddd ** (0.6 * r1a0 ** 0.9)).reshape(1, 1, C).astype(np.float32)
        lam = np.stack([1.0 - ddd ** (0.9 * r1a0), 1.0 - ddd ** (0.9 * r1a0) - 0.4 * r01, 1.0 - ddd ** (0.4 * r1a0) - 0.6 * r01, 1.0 - ddd ** (0.2 * r1a0), 1.0 - ddd ** (0.2 * r1a0)]).reshape(5, 1, 1, C).astype(np.float32)
        n = np.arange(C, dtype=np.float64)
        td_miu = (-6.0 + 5.5 * (n / (C - 1)) ** (0.85 + 1.0 * r01 ** 0.5)).reshape(1, 1, C).astype(np.float32)
        zigzag = ((n + 1) % 3 - 1) * 0.1
        u = (r01 * (2.5 - n / (C - 1)) + zigzag).reshape(N, HEAD).astype(np.float32)
        ks = jax.random.split(key, 12)
        unif = lambda k, shape, s: jax.random.uniform(k, shape, jnp.float32, -s, s)
        x = jax.random.normal(ks[0], (B, T, C), jnp.float32)
        return {'x': x, 'miu_x': jnp.asarray(miu_x), 'lam': jnp.asarray(lam), 'A': unif(ks[1], (C, 160), 0.01), 'Bp': unif(ks[2], (5, 32, C), 0.01), 'td_miu': jnp.asarray(td_miu), 'tdA': unif(ks[3], (C, 64), 0.01), 'tdB': unif(ks[4], (64, C), 0.01), 'u': jnp.asarray(u), 'Wk': unif(ks[5], (C, C), 0.05 / C ** 0.5), 'Wv': unif(ks[6], (C, C), 0.5 / C ** 0.5), 'Wr': unif(ks[7], (C, C), 0.5 / C ** 0.5), 'Wo': unif(ks[8], (C, C), 0.5 / C ** 0.5), 'Wg1': unif(ks[9], (C, 160), 0.01), 'Wg2': unif(ks[10], (160, C), 0.01), 'gamma': jnp.ones((C,), jnp.float32), 'beta': jnp.zeros((C,), jnp.float32)}
    _L0_attn_in = _L0_attn_setup()

    def _L0_ffn_setup():
        import jax, jax.numpy as jnp
        import numpy as np
        B, S, D, H, E = (4, 512, 256, 512, 8)
        key = jax.random.key(seed)
        ks = jax.random.split(key, 8)
        scale = 0.02
        return {'x': jax.random.normal(ks[0], (B, S, D), dtype=jnp.float32), 'Wr': jax.random.normal(ks[1], (D, E), dtype=jnp.float32) * scale, 'br': jnp.zeros((E,), dtype=jnp.float32), 'W1': jax.random.normal(ks[2], (E, D, H), dtype=jnp.float32) * scale, 'b1': jnp.zeros((E, H), dtype=jnp.float32), 'W2': jax.random.normal(ks[3], (E, H, D), dtype=jnp.float32) * scale, 'b2': jnp.zeros((E, D), dtype=jnp.float32)}
    _L0_ffn_in = _L0_ffn_setup()
    _d = {'L0_attn_x': _L0_attn_in['x'], 'L0_attn_miu_x': _L0_attn_in['miu_x'], 'L0_attn_lam': _L0_attn_in['lam'], 'L0_attn_A': _L0_attn_in['A'], 'L0_attn_Bp': _L0_attn_in['Bp'], 'L0_attn_td_miu': _L0_attn_in['td_miu'], 'L0_attn_tdA': _L0_attn_in['tdA'], 'L0_attn_tdB': _L0_attn_in['tdB'], 'L0_attn_u': _L0_attn_in['u'], 'L0_attn_Wk': _L0_attn_in['Wk'], 'L0_attn_Wv': _L0_attn_in['Wv'], 'L0_attn_Wr': _L0_attn_in['Wr'], 'L0_attn_Wo': _L0_attn_in['Wo'], 'L0_attn_Wg1': _L0_attn_in['Wg1'], 'L0_attn_Wg2': _L0_attn_in['Wg2'], 'L0_attn_gamma': _L0_attn_in['gamma'], 'L0_attn_beta': _L0_attn_in['beta'], 'L0_ffn_Wr': _L0_ffn_in['Wr'], 'L0_ffn_br': _L0_ffn_in['br'], 'L0_ffn_W1': _L0_ffn_in['W1'], 'L0_ffn_b1': _L0_ffn_in['b1'], 'L0_ffn_W2': _L0_ffn_in['W2'], 'L0_ffn_b2': _L0_ffn_in['b2']}
    _x0 = _d['L0_attn_x']
    _d['L0_attn_x'] = jax.random.normal(jax.random.fold_in(jax.random.key(seed), 1), (4, 1024, 256), dtype=_x0.dtype)
    del _x0
    return _d

def reference(L0_attn_x, L0_attn_miu_x, L0_attn_lam, L0_attn_A, L0_attn_Bp, L0_attn_td_miu, L0_attn_tdA, L0_attn_tdB, L0_attn_u, L0_attn_Wk, L0_attn_Wv, L0_attn_Wr, L0_attn_Wo, L0_attn_Wg1, L0_attn_Wg2, L0_attn_gamma, L0_attn_beta, L0_ffn_Wr, L0_ffn_br, L0_ffn_W1, L0_ffn_b1, L0_ffn_W2, L0_ffn_b2):

    def _L0_attn_ref(x, miu_x, lam, A, Bp, td_miu, tdA, tdB, u, Wk, Wv, Wr, Wo, Wg1, Wg2, gamma, beta):
        import jax, jax.numpy as jnp
        import numpy as np
        HEAD = 64

        def wkv6(r, k, v, w, u):
            B, T, C = r.shape
            N = C // HEAD
            shp = lambda a: a.reshape(B, T, N, HEAD).transpose(1, 0, 2, 3)
            rT, kT, vT = (shp(r), shp(k), shp(v))
            dT = jnp.exp(shp(w))
            uu = u[None]

            def step(S, inp):
                rt, kt, vt, dt = inp
                kv = vt[..., :, None] * kt[..., None, :]
                yt = jnp.einsum('bnj,bnij->bni', rt, S + uu[..., None, :] * kv)
                S = S * dt[..., None, :] + kv
                return (S, yt)
            S0 = jnp.zeros((B, N, HEAD, HEAD), r.dtype)
            _, ys = jax.lax.scan(step, S0, (rT, kT, vT, dT))
            return ys.transpose(1, 0, 2, 3).reshape(B, T, C)
        B, T, C = x.shape
        N = C // HEAD
        x_last = jnp.concatenate([jnp.zeros_like(x[:, :1]), x[:, :-1]], axis=1)
        b_a = x_last - x
        xx = x + b_a * miu_x
        h = jnp.tanh(xx @ A).reshape(5, B * T, 32)
        miu = jnp.einsum('smk,skc->smc', h, Bp).reshape(5, B, T, C) + lam
        x5 = x[None] + b_a[None] * miu
        w_in, k_in, v_in, r_in, g_in = (x5[0], x5[1], x5[2], x5[3], x5[4])
        w = td_miu + jnp.tanh(w_in @ tdA) @ tdB
        k = k_in @ Wk.T * jnp.exp(jnp.minimum(w, 0.0))
        v = v_in @ Wv.T
        r = r_in @ Wr.T
        g = jnp.tanh(g_in @ Wg1) @ Wg2
        y = wkv6(r, k, v, w, u)
        yh = y.reshape(B, T, N, HEAD)
        mean = yh.mean(-1, keepdims=True)
        var = yh.var(-1, keepdims=True)
        yn = (yh - mean) / jnp.sqrt(var + 1e-05 * N)
        yn = yn.reshape(B, T, C) * gamma + beta
        return yn * g @ Wo.T

    def _L0_ffn_ref(x, Wr, br, W1, b1, W2, b2):
        import jax, jax.numpy as jnp
        import numpy as np
        B, S, D, H, E = (4, 512, 256, 512, 8)
        d = x.shape[-1]
        tokens = x.reshape(-1, d)
        logits = tokens @ Wr + br
        probs = jax.nn.softmax(logits, axis=-1)
        expert = jnp.argmax(probs, axis=-1)
        max_prob = jnp.take_along_axis(probs, expert[:, None], axis=-1)
        h = jax.nn.relu(jnp.einsum('td,edh->teh', tokens, W1) + b1[None])
        y = jnp.einsum('teh,ehd->ted', h, W2) + b2[None]
        out = jnp.take_along_axis(y, expert[:, None, None], axis=1)[:, 0, :]
        return (out * max_prob).reshape(x.shape)
    x = L0_attn_x
    xn = _layernorm(x, axis=-1)
    x = x + _L0_attn_ref(xn, L0_attn_miu_x, L0_attn_lam, L0_attn_A, L0_attn_Bp, L0_attn_td_miu, L0_attn_tdA, L0_attn_tdB, L0_attn_u, L0_attn_Wk, L0_attn_Wv, L0_attn_Wr, L0_attn_Wo, L0_attn_Wg1, L0_attn_Wg2, L0_attn_gamma, L0_attn_beta) + _L0_ffn_ref(xn, L0_ffn_Wr, L0_ffn_br, L0_ffn_W1, L0_ffn_b1, L0_ffn_W2, L0_ffn_b2)
    return x

_drawn_inputs = setup_inputs


def setup_inputs(seed=0):
    import zlib

    import numpy as np

    out = dict(_drawn_inputs(seed))
    spreads = {'L0_attn_gamma': (1.0, 0.6),
     'L0_attn_beta': (0.0, 0.8),
     'L0_ffn_br': (0.0, 0.34),
     'L0_ffn_b1': (0.0, 0.8),
     'L0_ffn_b2': (0.0, 0.393)}
    factors = {'L0_attn_miu_x': 8.0,
     'L0_attn_lam': 8.0,
     'L0_attn_A': 8.0,
     'L0_attn_Bp': 8.0,
     'L0_attn_td_miu': 8.0,
     'L0_attn_tdA': 8.0,
     'L0_attn_tdB': 8.0,
     'L0_attn_u': 8.0,
     'L0_attn_Wk': 8.0,
     'L0_attn_Wv': 8.0,
     'L0_attn_Wr': 8.0,
     'L0_attn_Wo': 8.0,
     'L0_attn_Wg1': 8.0,
     'L0_attn_Wg2': 8.0,
     'L0_ffn_W1': 3.218}
    for name, (base, spread) in spreads.items():
        noise = np.random.default_rng([zlib.crc32(name.encode()), seed]).standard_normal(out[name].shape)
        drawn = base * np.exp(spread * noise) if base else spread * noise
        out[name] = jnp.asarray(drawn.astype(out[name].dtype))
    for name, factor in factors.items():
        out[name] = (out[name] * factor).astype(out[name].dtype)
    return out
```

```python
from contextlib import ExitStack

import numpy as np
import concourse.bass as bass
from concourse import mybir

F32 = mybir.dt.float32
I32 = mybir.dt.int32
U32 = mybir.dt.uint32
ALU = mybir.AluOpType
ACT = mybir.ActivationFunctionType
AX = mybir.AxisListType

P = 128
NB, T, C = 4, 1024, 256
TOK = NB * T
CC = C // P
HEAD = 64
H2 = P // HEAD
NT = TOK // P
NCH = T // P
HID, E = 512, 8
HC = HID // P
LORA, NS = 32, 5
GR = NS * LORA
TDR = 64
GROUPS = CC * H2
NV = NB * GROUPS
EPS_LN = 1e-5
EPS_GN = 1e-5 * GROUPS
LEAF = 32
LEVELS = [0, 1, 2, 4, 8, 16]
FT = -(-(TOK + E * (P - 1)) // P)
FPI = -(-FT // NCH)
FT = FPI * NCH

MX, TDM, UU, GAM, BET, LAM = [CC * n for n in range(6)]
NVEC = LAM + CC * NS
IDN, BLK = 0, P
NCONST = 2 * P
TRI, ONE = 0, P
RANK8 = 2 * P
TILE_AT = RANK8 + E * NT
TILE_NO = TILE_AT + E * NT
NROUTE = TILE_NO + FT * (E - 1)


class Flow:

    def __init__(self, nc, sems, known):
        self.nc, self.sems, self.known = nc, sems, known
        self.count = {e: 0 for e in sems}
        self.table, self.per_turn = {}, {}
        self.loop, self.i = None, None
        self.turns, self.seen = {}, {}
        self.lead = {e: 0 for e in sems}
        if known:
            for e in sems:
                most = max([k.get(e, 0) for k in known["per_turn"].values()] + [0])
                self.lead[e] = most
                if most:
                    engine_of(nc, e).sem_inc(sems[e], most)

    def done(self, e, name, ins):
        ins.then_inc(self.sems[e], 1)
        self.count[e] += 1
        self.table[name] = (e, self.count[e], self.loop)
        return ins

    def wait(self, eng, *names):
        if not self.known:
            return
        need = {}
        for name in names:
            name, lag = name if isinstance(name, tuple) else (name, 0)
            e, c, loop = self.known["table"][name]
            c += self.lead[e]
            k = self.known["per_turn"].get(loop, {}).get(e, 0)
            if loop is not None and loop == self.loop:
                turning, c = True, c - lag * k
            else:
                turning = False
                if loop is not None:
                    c += (self.known["turns"][loop] - 1 - lag) * k
            need[e, turning] = max(need.get((e, turning), 0), c)
        for (e, turning), c in need.items():
            key = (eng.engine, e, turning)
            if self.seen.get(key, -1) >= c:
                continue
            self.seen[key] = c
            if turning:
                eng.wait_ge(self.sems[e], self.i * self.known["per_turn"][self.loop][e] + c)
            else:
                eng.wait_ge(self.sems[e], c)

    def start_loop(self, name, turns, i):
        self.loop, self.i = name, i
        self.seen = {}
        self.turns[name] = turns
        self.before = dict(self.count)

    def end_loop(self):
        k = {e: self.count[e] - self.before[e] for e in self.count}
        self.per_turn[self.loop] = k
        for e in k:
            self.count[e] = self.before[e] + k[e] * self.turns[self.loop]
        self.loop, self.i = None, None
        self.seen = {}

    def known_after(self):
        return {"table": self.table, "per_turn": self.per_turn, "turns": self.turns}


def engine_of(nc, e):
    return {"pe": nc.tensor, "dve": nc.vector, "act": nc.scalar, "pool": nc.gpsimd}[e]


def program(nc, io, known):
    pe, dve, act, pool, sp = nc.tensor, nc.vector, nc.scalar, nc.gpsimd, nc.sync
    with ExitStack() as ctx:
        def sb(name, shape, dt=F32):
            return ctx.enter_context(nc.sbuf_tensor(name, shape, dt))

        def sem(name):
            return ctx.enter_context(nc.semaphore(name))

        xnT = sb("xnT", [P, CC, NB, T + 1])
        hT = sb("hT", [P, TOK])
        hT4 = sb("hT4", [P, T])
        w1 = sb("w1", [P, E * CC * HID])
        w2 = sb("w2", [P, E * HC * C])
        b2r = sb("b2r", [P, E * C])
        b1c = sb("b1c", [P, E * HC])
        bpz = sb("bpz", [P, 4, C])
        bp4z = sb("bp4z", [P, NB, C])
        tdA = sb("tdA", [P, CC, TDR])
        tdB = sb("tdB", [TDR, C])
        wk, wr, wv, wo = (sb(n, [P, CC, C]) for n in ("wk", "wr", "wv", "wo"))
        wg1 = sb("wg1", [P, CC, GR])
        wg2 = sb("wg2", [P, 2, C])
        vec = sb("vec", [P, NVEC])
        con = sb("con", [P, NCONST])
        msk = sb("msk", [P, len(LEVELS), LEAF], U32)
        brc = sb("brc", [E, 1])
        S = sb("S", [P, CC * NB, HEAD])
        slot = sb("slot", [P, NT], I32)
        prob = sb("prob", [P, NT])
        expert = sb("expert", [1, FT], I32)
        small = sb("small", [P, 64])

        ba = sb("ba", [P, CC, NB, P])
        mix = [sb("mix0", [P, CC, NB, P]), sb("mix1", [P, CC, NB, P])]
        R = sb("R", [P, CC, NB, P])
        K = sb("K", [P, CC, NB, P])
        D = sb("D", [P, 2 * CC * NB * P])
        V = sb("V", [P, NB, C])
        tg = sb("tg", [P, 2, NB * P])
        tw = sb("tw", [TDR, NB * P])
        AT = sb("AT", [P, CC, H2, NB, P])
        AP_ = sb("AP_", [P, CC, H2, NB, LEAF])
        res = sb("res", [P, NB, C])
        xs = sb("xs", [P, C])
        xsT = sb("xsT", [P, CC, P])
        hs = sb("hs", [P, HID])
        hsT = sb("hsT", [P, HC, P])
        ys = hs[:, 0:C]

        xx = w1[:, 0:CC * TOK].rearrange("p (c n) -> p c n", c=CC)
        xtok = w2[:, 0:NT * C].rearrange("p (n c) -> p n c", n=NT)
        logT = hs

        PS = [ctx.enter_context(nc.psum_tensor(f"PS{n}", [P, 512], F32)) for n in range(8)]
        G = PS[0:2]
        FA, FB = PS[2], PS[3]
        L = [[PS[4], PS[5]], [PS[6], PS[7]]]

        xs_d = nc.dram_tensor("xs_d", [FT * P, C], F32, kind="Internal").ap()
        ys_d = nc.dram_tensor("ys_d", [FT * P, C], F32, kind="Internal").ap()
        at_d = nc.dram_tensor("at_d", [TOK, C], F32, kind="Internal").ap()
        lg_d = nc.dram_tensor("lg_d", [E, TOK], F32, kind="Internal").ap()

        sems = {"pe": sem("pe_done"), "dve": sem("dve_done"), "act": sem("act_done"), "pool": sem("pool_done")}
        q_con, q_w, q_x, q_zero, q_scat, q_ew, q_xs, q_ys, q_res, q_at, q_fin, q_gat, q_out, q_al, q_lg, q_l2 = (
            sem(n) for n in ("q_con", "q_w", "q_x", "q_zero", "q_scat", "q_ew", "q_xs", "q_ys", "q_res", "q_at",
                             "q_fin", "q_gat", "q_out", "q_al", "q_lg", "q_l2"))
        gn3 = sb("gn3", [P, 3, NV])
        gv, gy, ga = (gn3[:, n, :] for n in range(3))
        carrier = sem("carrier")
        fl = Flow(nc, sems, known)
        for q in (q_ys, q_at, q_out):
            sp.sem_inc(q, LEADQ)
        done, wait = fl.done, fl.wait

        ident = con[:, IDN:IDN + P]

        def settle(eng):
            eng.sem_inc(carrier, 1)

        def cvec(col, cc):
            return vec[:, col + cc:col + cc + 1]

        rout = D[:, 0:NROUTE]
        small_loads = [
            (con[:, :], io["con"]), (rout, io["rout"]), (vec[:, :], io["vec"]), (brc[:, :], io["br"]), (msk[:, :, :], io["msk"]),
            (xn_A := tg[:, 0, 0:CC * GR].rearrange("p (c n) -> p c n", c=CC), io["A"].rearrange("(c p) n -> p c n", p=P)),
            (tdA[:, :, :], io["tdA"].rearrange("(c p) n -> p c n", p=P)),
            (tdB[:, :], io["tdB"]),
            (wk[:, :, :], io["WkT"].rearrange("(c p) n -> p c n", p=P)),
            (wr[:, :, :], io["WrT"].rearrange("(c p) n -> p c n", p=P)),
            (wv[:, :, :], io["WvT"].rearrange("(c p) n -> p c n", p=P)),
            (wo[:, :, :], io["WoT"].rearrange("(c p) n -> p c n", p=P)),
            (wg1[:, :, :], io["Wg1"].rearrange("(c p) n -> p c n", p=P)),
            (wg2[:, 0, :], io["Wg2"][0:P, :]), (wg2[0:GR - P, 1, :], io["Wg2"][P:GR, :]),
            (tw[:, 0:0 + 1], None),
            (b1c[:, :], io["b1c"]),
        ]
        wrt = tg[:, 1, 0:CC * E].rearrange("p (c n) -> p c n", c=CC)
        small_loads = [x for x in small_loads if x[1] is not None]
        small_loads.append((wrt, io["Wr"].rearrange("(c p) n -> p c n", p=P)))
        for dst, src in small_loads:
            sp.dma_start(dst, src).then_inc(q_con, 16)
        N_CON = 16 * len(small_loads)

        mhalf = small[:, 59:60]
        done("pool", "mhalf", pool.memset(mhalf, -0.5))
        wait(pool, "mhalf")
        Z = hs
        done("pool", "z_hs", pool.memset(Z[:, :], 0.0))
        wait(sp, "z_hs")
        zsrc = Z[:, :].rearrange("p (a c) -> p a c", c=C)
        for n in range(FT // 2):
            sp.dma_start(xs_d[n * 2 * P:(n + 1) * 2 * P, :].rearrange("(p a) c -> p a c", a=2), zsrc).then_inc(q_zero, 16)
        N_ZERO = 16 * (FT // 2)
        done("pool", "z_bpz", pool.memset(bpz[:, :, :], 0.0))
        done("pool", "z_bp4", pool.memset(bp4z[:, :, :], 0.0))
        done("pool", "z_x0", pool.memset(xnT[:, :, :, 0:1], 0.0))
        pool.memset(S[:, :, :], 0.0)
        pool.memset(AT[:, :, :, :, :], 0.0)
        done("pool", "z_all", pool.memset(AP_[:, :, :, :, :], 0.0))
        wait(act, "z_bp4")
        for s in range(4):
            act.dma_start(bpz[LORA * s:LORA * (s + 1), s, :], io["Bp"][s]).then_inc(q_w, 16)
        for b in range(NB):
            act.dma_start(bp4z[LORA * b:LORA * (b + 1), b, :], io["Bp"][4]).then_inc(q_w, 16)
        act.dma_start(b2r[:, :], io["b2"].partition_broadcast(P)).then_inc(q_w, 16)
        N_W = 16 * 9

        def rsqrt(v, y, a, name):
            def to(tag, ins):
                done("dve", f"{name}{tag}", ins)
                wait(dve, f"{name}{tag}")
            to("_h", dve.tensor_scalar(a.bitcast(I32), v.bitcast(I32), 1, None, ALU.logical_shift_right))
            to("_g", dve.tensor_scalar(y.bitcast(I32), a.bitcast(I32), -1.0, float(0x5f3759df), ALU.mult, ALU.add))
            for n in range(3):
                to(f"_a{n}", dve.scalar_tensor_tensor(a, y, -0.5, y, ALU.mult, ALU.mult))
                to(f"_b{n}", dve.tensor_tensor(a, a, v, ALU.mult))
                to("" if n == 2 else f"_y{n}", dve.scalar_tensor_tensor(y, a, 1.5, y, ALU.add, ALU.mult))

        xin = ba[:, :, :, :].rearrange("p c b n -> p (c b n)").rearrange("p (t c) -> p t c", c=C)
        xdr = io["x"].rearrange("(b h t p) c -> b h p t c", b=NB, h=2, t=4)
        st = small[:, 0:24].rearrange("p (t s) -> p t s", t=4)
        mv = small[:, 24:32].rearrange("p (t s) -> p t s", t=4)
        rs = small[:, 32:36]
        for e in (dve, pe, act):
            e.wait_ge(q_con, N_CON)
        wait(dve, "z_x0")
        with nc.Fori(0, NB) as b:
            fl.start_loop("ln", NB, b)
            for hf in range(2):
                t0 = 4 * hf
                wait(sp, ("xn1" if hf == 0 else "xn0", 1 if hf == 0 else 0))
                sp.dma_start(xin, xdr[bass.ds(b, 1), hf, :, :, :]).then_inc(q_x, 16)
                dve.wait_ge(q_x, b * 32 + 16 * (hf + 1))
                for t in range(4):
                    i1 = dve.bn_stats(st[:, t, :], xin[:, t, :])
                done("dve", f"bn{hf}", i1)
                wait(dve, f"bn{hf}")
                settle(dve)
                for t in range(4):
                    i1 = dve.bn_aggr(mv[:, t, :], st[:, t, :])
                done("dve", f"ag{hf}", i1)
                wait(dve, f"ag{hf}")
                done("dve", f"ve{hf}", dve.tensor_scalar(rs, mv[:, :, 1], EPS_LN, None, ALU.add))
                wait(pool, f"ve{hf}")
                done("pool", f"rs{hf}", pool.tensor_tensor(rs, rs, mhalf[:, 0:1].broadcast_to([P, 4]), ALU.pow))
                wait(dve, f"rs{hf}")
                for t in range(4):
                    i1 = dve.tensor_scalar(xtok[:, bass.ds(b * 8 + (t0 + t), 1), :].rearrange("p o c -> p (o c)"), xin[:, t, :], mv[:, t, 0:1], rs[:, t:t + 1],
                                           ALU.subtract, ALU.mult)
                    i2 = dve.tensor_scalar(res[:, t, :], xin[:, t, :], mv[:, t, 0:1], rs[:, t:t + 1],
                                           ALU.subtract, ALU.mult)
                done("dve", f"xn{hf}", i2)
                wait(pe, f"xn{hf}", (f"tc{1 - hf}", 1 - hf))
                for cc in range(CC):
                    for t in range(4):
                        i1 = pe.transpose(L[cc][0][:, P * t:P * (t + 1)], res[:, t, cc * P:(cc + 1) * P], ident)
                done("pe", f"tr{hf}", i1)
                wait(act, f"tr{hf}")
                for cc in range(CC):
                    i1 = act.activation(xnT[:, cc, bass.ds(b, 1), 1 + 512 * hf:1 + 512 * (hf + 1)].rearrange("p o n -> p (o n)"), L[cc][0][:, :], ACT.Copy)
                done("act", f"tc{hf}", i1)
                wait(pe, f"tc{hf}", (f"lgc{1 - hf}", 1 - hf))
                for cc in range(CC):
                    i1 = pe.matmul(FA[0:E, :], wrt[:, cc, :], xnT[:, cc, bass.ds(b, 1), 1 + 512 * hf:1 + 512 * (hf + 1)].rearrange("p o n -> p (o n)"),
                                   start=(cc == 0), stop=(cc == CC - 1))
                done("pe", f"lg{hf}", i1)
                wait(act, f"lg{hf}")
                if hf == 0:
                    act.wait_ge(q_zero, N_ZERO)
                    act.wait_ge(q_lg, b * 32 + 1 - 1) if False else None
                done("act", f"lgc{hf}", act.activation(mix[0][0:E, hf, :, :].rearrange("p b n -> p (b n)"), FA[0:E, :], ACT.Identity, bias=brc[:, 0:1]))
                wait(sp, f"lgc{hf}")
                sp.dma_start(lg_d[:, bass.ds(b * T + 512 * hf, 512)], mix[0][0:E, hf, :, :].rearrange("p b n -> p (b n)")).then_inc(q_lg, 16)
                act.wait_ge(q_lg, b * 32 + 16 * (hf + 1))
            wait(dve, "tc1")
            xb = xnT[:, :, bass.ds(b, 1), :].rearrange("p c o n -> p c (o n)")
            xo = xx[:, :, bass.ds(b * T, T)]
            done("dve", "xd", dve.tensor_tensor(xo, xb[:, :, 0:T], xb[:, :, 1:T + 1], ALU.subtract))
            wait(dve, "xd")
            for cc in range(CC):
                i1 = dve.scalar_tensor_tensor(xx[:, cc, bass.ds(b * T, T)], xx[:, cc, bass.ds(b * T, T)], cvec(MX, cc), xnT[:, cc, bass.ds(b, 1), 1:T + 1].rearrange("p o n -> p (o n)"),
                                              ALU.mult, ALU.add)
            done("dve", "xx", i1)
            fl.end_loop()

        lg = mix[1][:, 0, 0:2, :].rearrange("p b n -> p (b n)").rearrange("p (t e) -> p t e", e=E)
        sp.wait_ge(q_lg, 16 * 2 * NB)
        lgt = R[:, 0, :, :].rearrange("p b n -> p (b n)")[0:NT * 4, :]
        lrow = [R[:, 0, n, :] for n in range(2)]
        for n in range(2):
            for t in range(NT // 2):
                sp.dma_start(R[E * t:E * (t + 1), 0, n, :], lg_d[:, (n * NT // 2 + t) * P:(n * NT // 2 + t + 1) * P]).then_inc(q_l2, 16)
        pe.wait_ge(q_l2, 16 * NT)
        wait(pe, "lgc1")
        for n in range(2):
            i1 = pe.transpose(FA[:, n * P:(n + 1) * P], lrow[n], ident)
        done("pe", "r_tr", i1)
        wait(dve, "r_tr")

        def area(n):
            return K[:, 0, :, :].rearrange("p b n -> p (b n)")[:, 256 * (n % 2):256 * (n % 2) + 256].rearrange("p (t e) -> p t e", e=E) if n < 2 else \
                K[:, 1, :, :].rearrange("p b n -> p (b n)")[:, 256 * (n % 2):256 * (n % 2) + 256].rearrange("p (t e) -> p t e", e=E)
        ex, oh, pre, tot = (area(n) for n in range(4))
        Lg = FA[:, 0:NT * E].rearrange("p (t e) -> p t e", e=E)
        m1 = small[:, 0:NT]

        def bc(a):
            return a.rearrange("p (t o) -> p t o", o=1).broadcast_to([P, NT, E])

        def step(name, ins):
            done("dve", name, ins)
            wait(dve, name)

        step("r_max", dve.tensor_reduce(m1, Lg, AX.X, ALU.max))
        step("r_sub", dve.tensor_tensor(ex, Lg, bc(m1), ALU.subtract))
        wait(act, "r_sub")
        done("act", "r_exp", act.activation(ex, ex, ACT.Exp))
        wait(dve, "r_exp")
        step("r_sum", dve.tensor_reduce(m1, ex, AX.X, ALU.add))
        step("r_rec", dve.reciprocal(m1, m1))
        step("r_prb", dve.tensor_tensor(ex, ex, bc(m1), ALU.mult))
        step("r_pmx", dve.tensor_reduce(prob[:, :], ex, AX.X, ALU.max))
        step("r_eq", dve.tensor_tensor(oh, ex, bc(prob[:, :]), ALU.is_equal))
        rank8 = rout[:, RANK8:RANK8 + NT * E].rearrange("p (t e) -> p t e", e=E)
        step("r_rk", dve.tensor_tensor(oh, oh, rank8, ALU.mult))
        step("r_rm", dve.tensor_reduce(m1, oh, AX.X, ALU.max))
        step("r_oh", dve.tensor_tensor(oh, rank8, bc(m1), ALU.is_equal))
        wait(pe, "r_oh")
        ohf = oh.rearrange("p t e -> p (t e)")
        pe.matmul(FA[:, 0:NT * E], rout[:, TRI:TRI + P], ohf, start=True, stop=True)
        done("pe", "r_mm", pe.matmul(FB[:, 0:NT * E], rout[:, ONE:ONE + P], ohf, start=True, stop=True))
        wait(dve, "r_mm")
        dve.tensor_copy(pre, FA[:, 0:NT * E].rearrange("p (t e) -> p t e", e=E))
        step("r_tot", dve.tensor_copy(tot, FB[:, 0:NT * E].rearrange("p (t e) -> p t e", e=E)))
        for e in range(E):
            i1 = dve.tensor_tensor_scan(ex[:, :, e], tot[:, :, e], tot[:, :, e], 0.0, ALU.add, ALU.bypass)
        step("r_scan", i1)
        cnt = ex[:, NT - 1, :]
        tl = small[:, 32:40]
        en = small[:, 40:48]
        cmp = AT[:, 0, 0, 0:2, :].rearrange("p b n -> p (b n)").rearrange("p (e j) -> p e j", e=E)
        tile_at = rout[:, TILE_AT:TILE_AT + E * NT].rearrange("p (e j) -> p e j", e=E)
        wait(dve, "z_all")
        step("r_cmp", dve.tensor_tensor(cmp, cnt.rearrange("p (e o) -> p e o", o=1).broadcast_to([P, E, NT]), tile_at, ALU.is_gt))
        step("r_tl", dve.tensor_reduce(tl, cmp, AX.X, ALU.add))
        step("r_en", dve.tensor_tensor_scan(en, tl, tl, 0.0, ALU.add, ALU.bypass))
        step("r_s0", dve.tensor_tensor(tl, en, tl, ALU.subtract))
        step("r_s1", dve.tensor_scalar(tl, tl, float(P), None, ALU.mult))
        step("r_s2", dve.tensor_tensor(pre, pre, ex, ALU.add))
        step("r_s3", dve.tensor_tensor(pre, pre, tot, ALU.subtract))
        step("r_s4", dve.tensor_tensor(pre, pre, tl.rearrange("p (o e) -> p o e", o=1).broadcast_to([P, NT, E]), ALU.add))
        step("r_s5", dve.tensor_tensor(pre, pre, oh, ALU.mult))
        step("r_s6", dve.tensor_reduce(m1, pre, AX.X, ALU.add))
        done("dve", "r_slot", dve.tensor_copy(slot[:, :], m1))
        tno = rout[0:1, TILE_NO:TILE_NO + FT * (E - 1)].rearrange("p (j e) -> p j e", e=E - 1)
        cm2 = R[0:1, 1, :, :].rearrange("p b n -> p (b n)")[:, 0:FT * (E - 1)].rearrange("p (j e) -> p j e", e=E - 1)
        ef = R[0:1, 1, :, :].rearrange("p b n -> p (b n)")[:, 300:300 + FT]
        step("r_c2", dve.tensor_tensor(cm2, tno, en[0:1, 0:E - 1].rearrange("p (o e) -> p o e", o=1).broadcast_to([1, FT, E - 1]), ALU.is_ge))
        step("r_ef", dve.tensor_reduce(ef, cm2, AX.X, ALU.add))
        step("r_ex", dve.tensor_copy(expert[:, :], ef))
        step("z_cmp", dve.memset(AT[:, 0, 0, 0:2, :], 0.0))
        wait(pool, "r_slot")
        pool.wait_ge(q_zero, N_ZERO)
        for t in range(NT):
            pool.indirect_dma_start(xs_d, bass.IndirectOffsetOnAxis(slot[:, t:t + 1], 0), xtok[:, t, :], None).then_inc(q_scat, 16)

        pieces = []
        for s in range(NS):
            if s < 4:
                for k in range(2):
                    pieces.append((s * TOK + k * TOK // 2, s * TOK + (k + 1) * TOK // 2, hT, s, s * TOK))
            else:
                for b4 in range(NB):
                    pieces.append((4 * TOK + b4 * T, 4 * TOK + (b4 + 1) * T, hT4, b4, 4 * TOK + b4 * T))
        for n, (q0, q1, dst, quad, base) in enumerate(pieces):
            n0, n1 = q0 // NS, -(-q1 // NS)
            w = n1 - n0
            b0, b1_ = L[n % 2]
            if n >= 2:
                wait(pe, f"h{n - 2}")
            if n == 0:
                wait(pe, "xx", "tc1")
            for cc in range(CC):
                pe.matmul(b0[:, 0:w], xn_A[:, cc, 0:P], xx[:, cc, n0:n1], start=(cc == 0), stop=(cc == 1))
            for cc in range(CC):
                i1 = pe.matmul(b1_[0:LORA, 0:w], xn_A[:, cc, P:GR], xx[:, cc, n0:n1], start=(cc == 0), stop=(cc == 1))
            done("pe", f"hm{n}", i1)
            wait(act, f"hm{n}")
            for g in range(NS):
                a0 = -(-(q0 - g) // NS)
                a1 = -(-(q1 - g) // NS)
                src = (b0[LORA * g:LORA * (g + 1), a0 - n0:a1 - n0] if g < 4 else b1_[0:LORA, a0 - n0:a1 - n0])
                m0 = NS * a0 + g - base
                i1 = act.activation(dst[LORA * quad:LORA * (quad + 1), m0:m0 + NS * (a1 - a0 - 1) + 1:NS], src, ACT.Tanh)
            done("act", f"h{n}", i1)
        LASTH = f"h{len(pieces) - 1}"
        LASTHM = f"hm{len(pieces) - 1}"

        mwv = small[:, 48:56]
        wv3 = wv[:, :, :].rearrange("p c (h i) -> p (c h) i", i=HEAD)
        step("wv_s", dve.tensor_reduce(mwv, wv3, AX.X, ALU.add))
        step("wv_m", dve.tensor_scalar(mwv, mwv, 1.0 / HEAD, None, ALU.mult))
        done("dve", "wv_c", dve.tensor_tensor(wv3, wv3, mwv.rearrange("p (g o) -> p g o", o=1).broadcast_to([P, CC * GROUPS, HEAD]), ALU.subtract))

        wait(sp, LASTHM)
        sp.wait_ge(q_scat, 16 * NT)
        for e in range(E):
            sp.dma_start(w1[:, e * CC * HID:(e + 1) * CC * HID].rearrange("p (c n) -> p c n", c=CC),
                         io["W1"][e].rearrange("(c p) n -> p c n", p=P)).then_inc(q_ew, 16)
            sp.dma_start(w2[:, e * HC * C:(e + 1) * HC * C].rearrange("p (c n) -> p c n", c=HC),
                         io["W2"][e].rearrange("(c p) n -> p c n", p=P)).then_inc(q_ew, 16)
        N_EW = 16 * 2 * E
        for e in (pe, dve):
            e.wait_ge(q_ew, N_EW)
            e.wait_ge(q_w, N_W)
        wait(pe, LASTH)
        wait(dve, "z_all")
        wait(pe, "wv_c")

        xres = io["x"].rearrange("(b k p) c -> k p b c", b=NB, k=NCH)
        aout = at_d.rearrange("(b k p) c -> k p b c", b=NB, k=NCH)
        NN = NB * P
        sq, yn, z = mix[0], mix[1], ba
        Ku, Kt = mix[1], mix[0]
        gT = D[:, 0:CC * NB * P].rearrange("p (c n) -> p c n", c=CC)

        def flat(a, cc):
            return a[:, cc, :, :].rearrange("p b n -> p (b n)")

        with nc.Fori(0, NCH) as c:
            fl.start_loop("main", NCH, c)
            gn = [0]

            def gbank(name):
                n = gn[0]
                gn[0] += 1
                users.append(name)
                return G[n % 2]

            users = []

            def free_bank(name):
                n = len(users)
                users.append(name)
                if n >= 2:
                    wait(pe, users[n - 2])
                else:
                    wait(pe, (known["ends"][n] if known else name, 1))
                return G[n % 2]

            wait(sp, ("out_last", 1))
            sp.wait_ge(q_at, c * 16 + 0) if False else None
            wait(dve, ("out_pe", 1))
            xc = xnT[:, :, :, bass.ds(c * P + 1, P)]
            xp = xnT[:, :, :, bass.ds(c * P, P)]
            done("dve", "ba", dve.tensor_tensor(ba[:, :, :, :], xp, xc, ALU.subtract))

            def mixed(s, buf, after):
                wait(dve, "ba")
                for cc in range(CC):
                    bank = free_bank(f"m{s}{cc}")
                    if s < 4:
                        i1 = pe.matmul(bank[:, :], bpz[:, s, cc * P:(cc + 1) * P],
                                       hT[:, :].rearrange("p (b n) -> p b n", b=NB)[:, :, bass.ds(c * P, P)], start=True, stop=True)
                    else:
                        for b in range(NB):
                            i1 = pe.matmul(bank[:, b * P:(b + 1) * P], bp4z[:, b, cc * P:(cc + 1) * P], hT4[:, bass.ds(c * P, P)],
                                           start=True, stop=True)
                    done("pe", f"mm{s}{cc}", i1)
                for cc in range(CC):
                    wait(dve, f"mm{s}{cc}", *(after or ()))
                    done("dve", f"m{s}{cc}", dve.scalar_tensor_tensor(
                        flat(buf, cc), G[(len(users) - CC + cc) % 2][:, :], vec[:, LAM + CC * s + cc:LAM + CC * s + cc + 1], flat(ba, cc), ALU.add, ALU.mult))
                    wait(dve, f"m{s}{cc}")
                    done("dve", f"x{s}{cc}", dve.tensor_tensor(buf[:, cc, :, :], buf[:, cc, :, :], xnT[:, cc, :, bass.ds(c * P + 1, P)], ALU.add))

            mixed(0, mix[0], None)
            bank = free_bank("tw")
            wait(pe, "x01")
            for cc in range(CC):
                i1 = pe.matmul(bank[0:TDR, :], tdA[:, cc, :], flat(mix[0], cc), start=(cc == 0), stop=(cc == 1))
            done("pe", "tA", i1)
            wait(act, "tA")
            done("act", "tw", act.activation(tw[:, :], bank[0:TDR, :], ACT.Tanh))
            mixed(1, mix[1], None)
            wait(pe, "tw")
            for cc in range(CC):
                bank = free_bank(f"d{cc}")
                done("pe", f"tB{cc}", pe.matmul(bank[:, :], tdB[:, cc * P:(cc + 1) * P], tw[:, :], start=True, stop=True))
                wait(act, f"tB{cc}")
                done("act", f"d{cc}", act.activation(D[:, cc * NN:(cc + 1) * NN], bank[:, :], ACT.Exp, bias=cvec(TDM, cc)))
            wait(pe, "x11")
            for co in range(CC):
                bank = free_bank(f"k{co}")
                for cc in range(CC):
                    i1 = pe.matmul(bank[:, :], wk[:, cc, co * P:(co + 1) * P], flat(mix[1], cc), start=(cc == 0), stop=(cc == 1))
                done("pe", f"km{co}", i1)
                wait(dve, f"km{co}", f"d{co}")
                done("dve", f"k{co}", dve.scalar_tensor_tensor(flat(K, co), D[:, co * NN:(co + 1) * NN], 1.0, bank[:, :], ALU.min, ALU.mult))
            mixed(2, mix[0], ("tA",))
            wait(pe, "x21")
            for bp in range(NB // 2):
                bank = free_bank(f"v{bp}")
                for b in (2 * bp, 2 * bp + 1):
                    for cc in range(CC):
                        i1 = pe.matmul(bank[:, (b % 2) * C:(b % 2 + 1) * C], mix[0][:, cc, b, :], wv[:, cc, :], start=(cc == 0), stop=(cc == 1))
                done("pe", f"vm{bp}", i1)
                wait(act, f"vm{bp}")
                done("act", f"v{bp}", act.activation(V[:, 2 * bp:2 * bp + 2, :].rearrange("p b n -> p (b n)"), bank[:, :], ACT.Copy))
            mixed(3, mix[1], ("km1",))
            wait(pe, "x31")
            for co in range(CC):
                bank = free_bank(f"r{co}")
                for cc in range(CC):
                    i1 = pe.matmul(bank[:, :], wr[:, cc, co * P:(co + 1) * P], flat(mix[1], cc), start=(cc == 0), stop=(cc == 1))
                done("pe", f"rm{co}", i1)
                wait(act, f"rm{co}")
                done("act", f"r{co}", act.activation(flat(R, co), bank[:, :], ACT.Copy))
            mixed(4, mix[0], ("vm1",))
            wait(pe, "x41")
            for k, (m0, m1_) in enumerate(((0, P), (P, GR))):
                bank = free_bank(f"tg{k}")
                for cc in range(CC):
                    i1 = pe.matmul(bank[0:m1_ - m0, :], wg1[:, cc, m0:m1_], flat(mix[0], cc), start=(cc == 0), stop=(cc == 1))
                done("pe", f"gm{k}", i1)
                wait(act, f"gm{k}")
                done("act", f"tg{k}", act.activation(tg[0:m1_ - m0, k, :], bank[0:m1_ - m0, :], ACT.Tanh))

            wait(act, "rm1", "k1")
            for cc in range(CC):
                done("act", f"ku{cc}", act.activation(flat(Ku, cc), flat(K, cc), ACT.Copy, scale=cvec(UU, cc)))

            def blocks(a, cc, B):
                return flat(a, cc).rearrange("p (n h t) -> p n h t", h=2, t=B)

            def tot_at(B):
                return 0 if B == 1 else sum(CC * NN // b for b in (1, 2, 4, 8, 16, 32, 64) if b < B)

            def tots(cc, B):
                n = NN // B
                o = tot_at(B) + cc * n
                return D[:, o:o + n]

            def grow(cc, B, tag):
                n = NN // (2 * B)
                tt = tots(cc, B).rearrange("p (n h) -> p n h", h=2)
                wide = lambda a: a.rearrange("p (n o) -> p n o", o=1).broadcast_to([P, n, B])
                dve_R = blocks(R, cc, B)[:, :, 1, :]
                dve_K = blocks(K, cc, B)[:, :, 0, :]
                dve.tensor_tensor(dve_R, dve_R, wide(tt[:, :, 0]), ALU.mult)
                dve.tensor_tensor(dve_K, dve_K, wide(tt[:, :, 1]), ALU.mult)
                done("dve", f"gr{tag}{cc}", dve.tensor_tensor(tots(cc, 2 * B), tt[:, :, 0], tt[:, :, 1], ALU.mult))

            for li, B in enumerate(LEVELS):
                for cc in range(CC):
                    if li == 0:
                        wait(pe, f"ku{cc}", f"r{cc}")
                    elif B > 1:
                        wait(pe, f"gr{B // 2}{cc}")
                    Ks = Ku if li == 0 else K
                    for h in range(H2):
                        if li == 0:
                            wait(pe, ("yg_last", 1), ("sq_last", 1))
                        else:
                            wait(pe, f"a{li - 1}{cc}{h}")
                        settle(pe)
                        for b in range(NB):
                            for q in range(P // LEAF):
                                i1 = pe.matmul(L[cc][h][LEAF * q:LEAF * (q + 1), b * LEAF:(b + 1) * LEAF],
                                               Ks[HEAD * h:HEAD * (h + 1), cc, b, LEAF * q:LEAF * (q + 1)],
                                               R[HEAD * h:HEAD * (h + 1), cc, b, LEAF * q:LEAF * (q + 1)],
                                               start=True, stop=True, tile_position=(HEAD * h, LEAF * q))
                        done("pe", f"l{li}{cc}{h}", i1)
                    for h in range(H2):
                        wait(dve, f"l{li}{cc}{h}")
                        if li == 0:
                            wait(dve, ("exp_last", 1))
                        else:
                            wait(dve, f"a{li - 1}{cc}{h}")
                        settle(dve)
                        m = msk[:, li:li + 1, :].broadcast_to([P, NB, LEAF])
                        done("dve", f"a{li}{cc}{h}", dve.copy_predicated(
                            AP_[:, cc, h, :, :], m, L[cc][h][:, 0:NB * LEAF].rearrange("p (b n) -> p b n", b=NB)))
                    if B >= 1:
                        if B == 1:
                            wait(dve, f"d{cc}")
                        else:
                            wait(dve, f"gr{B // 2}{cc}")
                        grow(cc, B, B)
            for B in (32, 64):
                for cc in range(CC):
                    wait(pe, f"gr{B // 2}{cc}")
                    for h in range(H2):
                        wait(pe, f"a{len(LEVELS) - 1}{cc}{h}" if B == 32 else f"e32{cc}{h}")
                        settle(pe)
                        for b in range(NB):
                            for s0 in range(0, P, 2 * B):
                                i1 = pe.matmul(L[cc][h][s0:s0 + B, b * B:(b + 1) * B], K[HEAD * h:HEAD * (h + 1), cc, b, s0:s0 + B],
                                               R[HEAD * h:HEAD * (h + 1), cc, b, s0 + B:s0 + 2 * B], start=True, stop=True,
                                               tile_position=(HEAD * h, s0))
                        done("pe", f"l{B}{cc}{h}", i1)
                    for h in range(H2):
                        wait(act, f"l{B}{cc}{h}")
                        if B == 32:
                            wait(act, ("y_last", 1))
                        for s0 in range(0, P, 2 * B):
                            i1 = act.activation(AT[s0:s0 + B, cc, h, :, s0 + B:s0 + 2 * B],
                                                L[cc][h][s0:s0 + B, 0:NB * B].rearrange("p (b n) -> p b n", b=NB), ACT.Copy)
                        done("act", f"e{B}{cc}{h}", i1)
                    wait(dve, f"gr{B // 2}{cc}", f"l{B}{cc}1")
                    grow(cc, B, B)
            for cc in range(CC):
                wait(act, f"a{len(LEVELS) - 1}{cc}0", f"a{len(LEVELS) - 1}{cc}1")
                for q in range(P // LEAF):
                    i1 = act.activation(AT[LEAF * q:LEAF * (q + 1), cc, :, :, LEAF * q:LEAF * (q + 1)].rearrange("p h b n -> p (h b) n"),
                                        AP_[LEAF * q:LEAF * (q + 1), cc, :, :, :].rearrange("p h b n -> p (h b) n"), ACT.Copy)
                done("act", f"sp{cc}" if cc == 0 else "exp_last", i1)

            wait(pe, "v1")
            for cc in range(CC):
                wait(pe, f"sp{cc}" if cc == 0 else "exp_last", f"e64{cc}1", f"gr64{cc}", ("S_new", 1))
                settle(pe)
                Y = L[cc][0]
                for b in range(NB):
                    for h in range(H2):
                        o = Y[HEAD * h:HEAD * (h + 1), b * P:(b + 1) * P]
                        vcol = slice(cc * P + h * HEAD, cc * P + (h + 1) * HEAD)
                        pe.matmul(o, V[:, b, vcol], AT[:, cc, h, b, :], start=True, stop=False, tile_position=(0, HEAD * h))
                        i1 = pe.matmul(o, S[HEAD * h:HEAD * (h + 1), cc * NB + b, :], R[HEAD * h:HEAD * (h + 1), cc, b, :],
                                       start=False, stop=True, tile_position=(HEAD * h, HEAD * h))
                done("pe", f"y{cc}" if cc == 0 else "y_last", i1)
            for cc in range(CC):
                bank = free_bank(f"kt{cc}")
                for b in range(NB):
                    i1 = pe.transpose(bank[:, b * P:(b + 1) * P], K[:, cc, b, :], ident)
                done("pe", f"kT{cc}", i1)
                wait(act, f"kT{cc}", "gm1")
                done("act", f"kt{cc}", act.activation(flat(Kt, cc), bank[:, :], ACT.Copy))
            bank = free_bank("S_new")
            wait(pe, "kt1")
            settle(pe)
            for cc in range(CC):
                for b in range(NB):
                    for h in range(H2):
                        i1 = pe.matmul(bank[HEAD * h:HEAD * (h + 1), (cc * NB + b) * HEAD:(cc * NB + b + 1) * HEAD],
                                       Kt[:, cc, b, HEAD * h:HEAD * (h + 1)], V[:, b, cc * P + h * HEAD:cc * P + (h + 1) * HEAD],
                                       start=True, stop=True, tile_position=(0, HEAD * h))
            done("pe", "sm", i1)
            wait(dve, "y_last")
            for cc in range(CC):
                i1 = dve.tensor_tensor(S[:, cc * NB:(cc + 1) * NB, :], S[:, cc * NB:(cc + 1) * NB, :],
                                       tots(cc, P).rearrange("p (n o) -> p n o", o=1).broadcast_to([P, NB, HEAD]), ALU.mult)
            done("dve", "S_dec", i1)
            wait(dve, "S_dec", "sm")
            done("dve", "S_new", dve.tensor_tensor(S[:, :, :].rearrange("p n i -> p (n i)"), S[:, :, :].rearrange("p n i -> p (n i)"), bank[:, :], ALU.add))

            vbank = free_bank("rs_v")
            for cc in range(CC):
                wait(act, f"y{cc}" if cc == 0 else "y_last", "sm")
                done("act", f"sq{cc}" if cc == 0 else "sq_last", act.activation(flat(sq, cc), L[cc][0][:, :], ACT.Square))
                wait(pe, f"sq{cc}" if cc == 0 else "sq_last")
                for b in range(NB):
                    o = (cc * NB + b) * H2
                    i1 = pe.matmul(vbank[:, o:o + H2], sq[:, cc, b, :], con[:, BLK:BLK + P:HEAD], start=True, stop=True)
            done("pe", "va", i1)
            wait(dve, "va")
            done("dve", "rs_v", dve.tensor_scalar(gv, vbank[:, 0:NV], EPS_GN, None, ALU.add))
            wait(dve, "rs_v")
            rsqrt(gv, gy, ga, "gn")
            for cc in range(CC):
                rstd = flat(yn, cc)
                bank = free_bank(f"rb{cc}")
                wait(pe, "gn")
                settle(pe)
                for b in range(NB):
                    o = (cc * NB + b) * H2
                    for h in range(H2):
                        i1 = pe.matmul(bank[HEAD * h:HEAD * (h + 1), b * P:(b + 1) * P], gy[:, o + h:o + h + 1].broadcast_to([P, HEAD]), ident,
                                       start=True, stop=True, tile_position=(0, HEAD * h))
                done("pe", f"rm_{cc}", i1)
                wait(act, f"rm_{cc}")
                done("act", f"rb{cc}", act.activation(rstd, bank[:, :], ACT.Copy))
                wait(dve, f"rb{cc}", f"sq{cc}" if cc == 0 else "sq_last")
                done("dve", f"yn{cc}" if cc == 0 else "yg_last", dve.tensor_tensor(rstd, L[cc][0][:, :], rstd, ALU.mult))
                wait(act, f"yn{cc}" if cc == 0 else "yg_last")
                done("act", f"yb{cc}", act.activation(rstd, rstd, ACT.Identity, bias=cvec(BET, cc), scale=cvec(GAM, cc)))
                bank = free_bank(f"z{cc}")
                wait(pe, "tg1")
                pe.matmul(bank[:, :], wg2[:, 0, cc * P:(cc + 1) * P], tg[:, 0, :], start=True, stop=False)
                done("pe", f"gg{cc}", pe.matmul(bank[:, :], wg2[0:GR - P, 1, cc * P:(cc + 1) * P], tg[0:GR - P, 1, :], start=False, stop=True))
                wait(dve, f"gg{cc}", f"yb{cc}")
                done("dve", f"z{cc}", dve.tensor_tensor(flat(z, cc), rstd, bank[:, :], ALU.mult))
            sp.wait_ge(q_at, c * 16 + 16)
            sp.dma_start(res[:, :, :], xres[bass.ds(c, 1), :, :, :]).then_inc(q_res, 16)
            wait(pe, "z1")
            dve.wait_ge(q_res, c * 16 + 16)
            for bp in range(NB // 2):
                bank = free_bank(f"o{bp}" if bp == 0 else "out_last")
                for b in (2 * bp, 2 * bp + 1):
                    for cc in range(CC):
                        i1 = pe.matmul(bank[:, (b % 2) * C:(b % 2 + 1) * C], z[:, cc, b, :], wo[:, cc, :], start=(cc == 0), stop=(cc == 1))
                done("pe", f"om{bp}" if bp == 0 else "out_pe", i1)
                wait(dve, f"om{bp}" if bp == 0 else "out_pe")
                r2 = res[:, 2 * bp:2 * bp + 2, :].rearrange("p b n -> p (b n)")
                done("dve", f"o{bp}" if bp == 0 else "out_last", dve.tensor_tensor(r2, r2, bank[:, :], ALU.add))
            wait(sp, "out_last")
            sp.dma_start(aout[bass.ds(c, 1), :, :, :], res[:, :, :]).then_inc(q_at, 16)

            for f in range(FPI):
                first, last = f == 0, f == FPI - 1
                prev = (lambda n: (f"{n}{FPI - 1}", 1)) if first else (lambda n: (f"{n}{f - 1}", 0))
                wait(sp, prev("fxt"))
                sp.dma_start(xs[:, :], xs_d[bass.ds((c * FPI + f) * P, P), :]).then_inc(q_xs, 16)
                pe.wait_ge(q_xs, c * (16 * FPI) + 16 * (f + 1))
                wait(pe, prev("fh"))
                for cc in range(CC):
                    i1 = pe.transpose(FA[:, cc * P:(cc + 1) * P], xs[:, cc * P:(cc + 1) * P], ident)
                done("pe", f"fxt{f}", i1)
                wait(act, f"fxt{f}", prev("fhm"))
                done("act", f"fx{f}", act.activation(xsT[:, :, :].rearrange("p c n -> p (c n)"), FA[:, 0:C], ACT.Copy))
                ev = pe.value_load(expert[0:1, bass.ds(c * FPI + f, 1)], min_val=0, max_val=E - 1)
                dv = dve.value_load(expert[0:1, bass.ds(c * FPI + f, 1)], min_val=0, max_val=E - 1)
                wait(pe, f"fx{f}", prev("fy"))
                for cc in range(CC):
                    i1 = pe.matmul(FB[:, :], xsT[:, cc, :], w1[:, bass.ds(ev * (CC * HID) + cc * HID, HID)], start=(cc == 0), stop=(cc == 1))
                done("pe", f"fhm{f}", i1)
                wait(act, f"fhm{f}", prev("fht"))
                act.wait_ge(q_ys, c * (16 * FPI) + 16 * f + LEADQ)
                done("act", f"fhc{f}", act.activation(hs[:, :], FB[:, :], ACT.Copy))
                wait(pe, f"fhc{f}")
                for k in range(HC):
                    i1 = pe.transpose(FA[:, k * P:(k + 1) * P], hs[:, k * P:(k + 1) * P], ident)
                done("pe", f"fht{f}", i1)
                wait(dve, f"fht{f}", prev("fym"))
                for k in range(HC):
                    i1 = dve.tensor_scalar(hsT[:, k, :], FA[:, k * P:(k + 1) * P], b1c[:, bass.ds(dv * HC + k, 1)], 0.0, ALU.add, ALU.max)
                done("dve", f"fh{f}", i1)
                wait(pe, f"fh{f}")
                for k in range(HC):
                    i1 = pe.matmul(FB[:, 0:C], hsT[:, k, :], w2[:, bass.ds(ev * (HC * C) + k * C, C)], start=(k == 0), stop=(k == HC - 1))
                done("pe", f"fym{f}", i1)
                wait(dve, f"fym{f}")
                done("dve", f"fy{f}", dve.tensor_tensor(ys[:, :], FB[:, 0:C], b2r[:, bass.ds(dv * C, C)], ALU.add))
                wait(sp, f"fy{f}")
                sp.dma_start(ys_d[bass.ds((c * FPI + f) * P, P), :], ys[:, :]).then_inc(q_ys, 16)
            fl.ends = [users[0::2][-1], users[1::2][-1]]
            fl.end_loop()

        dve.wait_ge(q_ys, 16 * FT + LEADQ)
        sp.wait_ge(q_at, 16 * NCH + 16)
        pool.wait_ge(q_ys, 16 * FT + LEADQ)
        adr = at_d.rearrange("(n t p) c -> n p t c", t=4, p=P)
        odr = io["out"].rearrange("(n t p) c -> n p t c", t=4, p=P)
        fa, fg = res, V
        wait(sp, "out_last")
        wait(pool, "sm")
        with nc.Fori(0, NT // 4) as n:
            fl.start_loop("end", NT // 4, n)
            sp.wait_ge(q_out, n * 16 + LEADQ)
            sp.dma_start(fa[:, :, :], adr[bass.ds(n, 1), :, :, :]).then_inc(q_fin, 16)
            wait(pool, ("fin", 1))
            done("pool", "ix", pool.tensor_copy(small[:, 60:64].bitcast(I32), slot[:, bass.ds(n * 4, 4)]))
            wait(pool, "ix")
            settle(pool)
            for t in range(4):
                pool.indirect_dma_start(fg[:, t, :], None, ys_d, bass.IndirectOffsetOnAxis(small[:, 60 + t:61 + t].bitcast(I32), 0)).then_inc(q_gat, 16)
            dve.wait_ge(q_fin, n * 16 + 16)
            dve.wait_ge(q_gat, n * 64 + 64)
            for t in range(4):
                i1 = dve.scalar_tensor_tensor(fa[:, t, :], fg[:, t, :], prob[:, bass.ds(n * 4 + t, 1)], fa[:, t, :], ALU.mult, ALU.add)
            done("dve", "fin", i1)
            wait(sp, "fin")
            sp.dma_start(odr[bass.ds(n, 1), :, :, :], fa[:, :, :]).then_inc(q_out, 16)
            fl.end_loop()
        sp.wait_ge(q_out, 16 * (NT // 4) + LEADQ)
        after = fl.known_after()
        after["ends"] = fl.ends
        return after


LEADQ = 16


def constants():
    con = np.zeros((P, NCONST), np.float32)
    con[:, IDN:IDN + P] = np.eye(P)
    a = np.arange(P)
    con[:, BLK:BLK + P] = (a[:, None] // HEAD == a[None] // HEAD) / HEAD
    rout = np.zeros((P, NROUTE), np.float32)
    rout[:, TRI:TRI + P] = a[:, None] < a[None]
    rout[:, ONE:ONE + P] = 1
    rout[:, RANK8:RANK8 + NT * E] = np.tile(E - np.arange(E), NT)
    rout[:, TILE_AT:TILE_AT + E * NT] = np.tile(P * np.arange(NT), E)
    rout[:, TILE_NO:] = np.repeat(np.arange(FT), E - 1)
    msk = np.zeros((P, len(LEVELS), LEAF), np.uint32)
    s, t = (a % LEAF)[:, None], np.arange(LEAF)[None]
    for n, B in enumerate(LEVELS):
        msk[:, n] = (s == t) if B == 0 else (s // (2 * B) == t // (2 * B)) & (s % (2 * B) < B) & (t % (2 * B) >= B)
    return con, rout, msk


def kernel(**inp):
    import concourse.bacc as _bacc
    from concourse.bass_utils import run_bass_kernel_spmd as _run

    g = {k.replace("L0_attn_", "a_").replace("L0_ffn_", "f_"): np.asarray(v) for k, v in inp.items()}
    con, rout, msk = constants()
    col = lambda v: v.reshape(-1, CC, P).transpose(2, 0, 1).reshape(P, -1)
    vec = np.concatenate([col(g[n]) for n in ("a_miu_x", "a_td_miu", "a_u", "a_gamma", "a_beta", "a_lam")], axis=1)
    arrays = {
        "x": g["a_x"].reshape(TOK, C), "con": con, "rout": rout, "msk": msk, "vec": vec,
        "A": g["a_A"], "Bp": g["a_Bp"], "tdA": g["a_tdA"], "tdB": g["a_tdB"],
        "WkT": g["a_Wk"].T, "WvT": g["a_Wv"].T, "WrT": g["a_Wr"].T, "WoT": g["a_Wo"].T,
        "Wg1": g["a_Wg1"], "Wg2": g["a_Wg2"], "Wr": g["f_Wr"], "br": g["f_br"].reshape(E, 1),
        "W1": g["f_W1"], "W2": g["f_W2"], "b1c": g["f_b1"].reshape(E * HC, P).T, "b2": g["f_b2"].reshape(E * C),
    }
    arrays = {k: np.ascontiguousarray(v) for k, v in arrays.items()}

    known = None
    for _ in range(2):
        nc = _bacc.Bacc("TRN2", target_bir_lowering=False, num_devices=1)
        io = {k: nc.dram_tensor(f"in_{k}", v.shape, mybir.dt.from_np(v.dtype), kind="ExternalInput").ap()
              for k, v in arrays.items()}
        io["out"] = nc.dram_tensor("out", (TOK, C), F32, kind="ExternalOutput").ap()
        known = program(nc, io, known)
    r = _run(nc, [{f"in_{k}": v for k, v in arrays.items()}], core_ids=[0])
    return r.results[0]["out"].reshape(NB, T, C)
```

```python
from contextlib import ExitStack

import numpy as np
import concourse.bass as bass
from concourse import mybir

F32 = mybir.dt.float32
F32R = mybir.dt.float32r
I32 = mybir.dt.int32
U32 = mybir.dt.uint32
ALU = mybir.AluOpType
ACT = mybir.ActivationFunctionType
AX = mybir.AxisListType

P = 128
NB, T, C = 4, 1024, 256
TOK = NB * T
CC = C // P
HEAD = 64
H2 = P // HEAD
NT = TOK // P
NCH = T // P
HID, E = 512, 8
HC = HID // P
LORA, NS = 32, 5
GR = NS * LORA
TDR = 64
GROUPS = CC * H2
NV = NB * GROUPS
EPS_LN = 1e-5
EPS_GN = 1e-5 * GROUPS
LEAF = 32
LEVELS = [0, 1, 2, 4, 8, 16]
UB = NB // 2
UN = UB * P
TURNS = NCH - 1
FT = (TOK + E * (P - 1)) // P
FPI = FT // TURNS

COST = {"ku": 0.95, "chi": 1.2, "clo": 1.4, "d": 1.1, "tg": 0.6, "tw": 0.3, "spread": 1.2, "ym": 1.3, "yb": 1.3,
        "m0": 0.8, "m1": 0.8, "m2": 0.8, "m3": 0.8, "m4": 0.8, "gr1": 0.9, "gr2": 0.9, "gr4": 0.8, "gr8": 0.7,
        "gr16": 0.7, "gr32": 0.7, "gr64": 0.7, "S_dec": 0.8, "x0": 1.2, "x1": 1.2, "x2": 1.2, "x3": 1.2, "x4": 1.2, "ba": 1.2, "gy": 0.8, "cr": 4.0, "res": 2.5}
WEIGHT = {"pe": 1.0, "dve": 1.0, "act": 0.8, "pool": 0.8, "sp": 0.3}

MX, TDM, UU, LAM = [CC * n for n in range(4)]
NVEC = LAM + CC * NS
IDN, TRI, ONE = 0, P, 2 * P
NCONST = 3 * P
RANK8 = 0
TILE_AT = RANK8 + E * NT
TILE_NO = TILE_AT + E * NT
NROUTE = TILE_NO + FT * (E - 1)
CODES = NS * TOK


class Flow:

    def __init__(self, nc, make_sem, known):
        self.nc, self.make_sem, self.known = nc, make_sem, known
        self.sems, self.count, self.table, self.per_turn, self.turns = {}, {}, {}, {}, {}
        self.stream, self.place, self.i, self.seen = "setup", "once", None, {}
        self.asked, self.clock, self.at, self.cost = None, {}, {}, 0.0
        if known:
            for key, lead in known["lead"].items():
                if lead:
                    nc.sync.sem_inc(self.sem(key), lead * self.unit(key))

    def unit(self, key):
        return 16 if key.startswith("q_") else 1

    def sem(self, key):
        if key not in self.sems:
            self.sems[key] = self.make_sem("s_" + key)
            self.count[key] = 0
        return self.sems[key]

    def done(self, e, name, ins):
        key = e if e.startswith("q_") else f"{self.stream}_{e}"
        ins.then_inc(self.sem(key), self.unit(key))
        self.count[key] += 1
        self.table[self.place, name] = (key, self.count[key])
        self.clock[e] = self.clock.get(e, 0.0) + (self.cost if e == "pe" else 2.5 if name[:2] in ("xs", "b2") else 1.1 if name[:2] == "fh" and e == "act" else COST.get(name.split(".")[0], 0.5))
        self.at[name] = self.clock[e]
        if e == "pe":
            self.cost = 0.0
        return ins

    def wait(self, eng, *names):
        ename = {"PE": "pe", "DVE": "dve", "Activation": "act", "Pool": "pool"}.get(str(eng.engine).split(".")[-1], "sp")
        for name in names:
            if not isinstance(name, tuple) or not name[1]:
                name = name if isinstance(name, str) else name[0]
                if self.asked is not None:
                    self.asked.append((name, ename))
                if name in self.at:
                    self.clock[ename] = max(self.clock.get(ename, 0.0), self.at[name] + 0.2)
        if not self.known:
            return
        need = {}
        for name in names:
            name, lag = name if isinstance(name, tuple) else (name, 0)
            assert lag or self.asked is None or (self.place, name) not in self.known["table"] or (self.place, name) in self.table, name
            if lag and self.place == "pre":
                continue
            place = {"last": "main"}.get(self.place, self.place) if lag else self.place
            if "/" in name:
                place, name = name.split("/")
            if (place, name) not in self.known["table"]:
                place = "once" if ("once", name) in self.known["table"] else "pre"
            key, c = self.known["table"][place, name]
            c += self.known["lead"].get(key, 0)
            k = self.known["per_turn"].get(place, {}).get(key, 0)
            if place == self.place:
                c -= lag * k
            elif k:
                c += (self.known["turns"][place] - max(lag, 1)) * k
            turning = bool(k) and place == self.place
            assert c > 0
            need[key, turning] = max(need.get((key, turning), 0), c)
        for (key, turning), c in need.items():
            mark = (eng.engine, key, turning)
            if self.seen.get(mark, -1) >= c:
                continue
            self.seen[mark] = c
            u = self.unit(key)
            if turning:
                eng.wait_ge(self.sem(key), self.i * (self.known["per_turn"][self.place][key] * u) + c * u)
            else:
                eng.wait_ge(self.sem(key), c * u)

    def enter(self, place, turns=1, i=None):
        self.place, self.i, self.seen = place, i, {}
        self.turns[place] = turns
        self.before = dict(self.count)

    def leave(self):
        if self.i is not None:
            k = {e: self.count[e] - self.before.get(e, 0) for e in self.count}
            self.per_turn[self.place] = {e: n for e, n in k.items() if n}
            for e, n in k.items():
                self.count[e] += n * (self.turns[self.place] - 1)
        self.place, self.i, self.seen = "once", None, {}

    def summary(self):
        lead = {}
        for k in self.per_turn.values():
            for e, n in k.items():
                if e not in ("q_fg0", "q_fg1"):
                    lead[e] = max(lead.get(e, 0), n)
        return {"table": self.table, "per_turn": self.per_turn, "turns": self.turns, "lead": lead, "steps": self.steps}


def program(nc, io, known):
    pe, dve, act, pool, sp = nc.tensor, nc.vector, nc.scalar, nc.gpsimd, nc.sync
    with ExitStack() as ctx:
        def sb(name, shape, dt=F32):
            return ctx.enter_context(nc.sbuf_tensor(name, shape, dt))

        def sem(name):
            return ctx.enter_context(nc.semaphore(name))

        xnT = sb("xnT", [P, CC, NB, T + 1])
        w1 = sb("w1", [P, E * CC * HID])
        w2 = sb("w2", [P, E * HC * C])
        b1c = sb("b1c", [P, E * HC])
        bst = sb("bst", [P, NS, C], F32R)
        tdA = sb("tdA", [P, CC, TDR])
        tdB = sb("tdB", [TDR, C])
        wk, wr, wv, wo = (sb(n, [P, CC, C]) for n in ("wk", "wr", "wv", "wo"))
        wg1 = sb("wg1", [P, CC, GR])
        wg2 = sb("wg2", [P, 2, C])
        vec = sb("vec", [P, NVEC])
        gab = sb("gab", [P, 2, C])
        con = sb("con", [P, NCONST])
        msk = sb("msk", [P, len(LEVELS), LEAF], U32)
        brc = sb("brc", [E, 1])
        S = sb("S", [P, 2, UB * CC, P])
        slot = sb("slot", [P, NT], I32)
        prob = sb("prob", [P, NT])
        expert = sb("expert", [1, FT], I32)
        small = sb("small", [P, 64])

        craw = sb("craw", [P, NS, UN])
        cd = sb("cd", [P, 2, NS, UN], F32R)
        mix = sb("mix", [P, 3, CC, UB, P])
        ba = sb("ba", [P, CC, UB, P])
        R = sb("R", [P, 2, CC, UB, P])
        K = sb("K", [P, 2, CC, UB, P])
        D = sb("D", [P, 2, 2 * CC * UN])
        V = sb("V", [P, 2, UB, C])
        tg = sb("tg", [P, 2, 2, UN])
        tw = sb("tw", [TDR, UN])
        AT = sb("AT", [P, 2, H2, CC, UB, P])
        AP_ = sb("AP_", [P, H2, CC, UB, LEAF])
        Ku = sb("Ku", [P, CC, UB, P])
        sq = sb("sq", [P, UB, C])
        yn = sb("yn", [P, UB, C])
        z = sb("z", [P, UB, C])
        Kt, zT = yn, sq
        res = sb("res", [P, 2, UB, C])
        xs = sb("xs", [P, 2, C])
        xsT = sb("xsT", [P, CC, P])
        hs = sb("hs", [P, HID])
        hsT = sb("hsT", [P, HC, P])
        ys = sb("ys", [P, C])
        b2t = sb("b2t", [P, 2, C])
        gn2 = sb("gn2", [P, 2, UB * GROUPS])
        gv, gy = (gn2[:, n, :] for n in range(2))

        PS = [ctx.enter_context(nc.psum_tensor(f"PS{n}", [P, 512], F32)) for n in range(8)]
        G = PS[0:2]
        FA, FB = PS[2], PS[3]
        L = PS[4:6]
        Y, BB = PS[6], PS[7]

        xs_d = nc.dram_tensor("xs_d", [FT * P, C], F32, kind="Internal").ap()
        ys_d = nc.dram_tensor("ys_d", [FT * P, C], F32, kind="Internal").ap()
        cd_d = nc.dram_tensor("cd_d", [LORA, CODES + P * NCH], F32, kind="Internal").ap()
        at_d = nc.dram_tensor("at_d", [TOK, C], F32, kind="Internal").ap()

        fl = Flow(nc, sem, known)
        done, wait = fl.done, fl.wait
        fl.steps = {}
        carrier = sem("carrier")

        def settle(eng):
            eng.sem_inc(carrier, 1)

        def interleave(tag, *streams):
            steps = {n: [] for n, _ in streams}
            old = known["steps"][fl.place, tag] if known else {n: [] for n, _ in streams}
            total = {n: sum(step[0] for step in old[n]) + 0.01 for n in old}
            spent = {n: 0.0 for n in old}
            live = dict(streams)
            fl.clock, fl.at = {}, {}
            while live:
                now = fl.clock.get("pe", 0.0)
                best = None
                for n in live:
                    k = len(steps[n])
                    stall = 0.0
                    if known and k < len(old[n]):
                        asked = old[n][k][1]
                        if any((fl.place, a) in known["table"] and (fl.place, a) not in fl.table and a not in old[n][k][2] for a, _ in asked):
                            continue
                        for a, e in asked:
                            if a in fl.at and a not in old[n][k][2]:
                                stall = max(stall, WEIGHT[e] * (fl.at[a] + 0.2 - max(now, fl.clock.get(e, 0.0))))
                    score = (max(stall - 0.3, 0.0), spent[n] / total[n])
                    if best is None or score < best[0]:
                        best = (score, n)
                n = best[1]
                fl.stream, fl.asked = n, []
                k = len(steps[n])
                fl.cost = old[n][k][0] if k < len(old[n]) else 0.0
                before = set(fl.table)
                try:
                    cost = next(live[n])
                except StopIteration:
                    cost = 0.0
                    del live[n]
                spent[n] += cost
                own = {a for p_, a in set(fl.table) - before}
                steps[n].append((cost, fl.asked, own))
            fl.asked = None
            fl.steps[fl.place, tag] = steps

        def cvec(col, cc):
            return vec[:, col + cc:col + cc + 1]

        ident = con[:, IDN:IDN + P]

        aT = AT[:, 0].rearrange("p h c b n -> p (h c b n)")
        aT1 = AT[:, 1].rearrange("p h c b n -> p (h c b n)")
        rout = aT1[:, 0:NROUTE]
        xin = [R[:, :, :, :, :].rearrange("p u c b n -> p (u c b n)").rearrange("p (t c) -> p t c", c=C),
               K[:, :, :, :, :].rearrange("p u c b n -> p (u c b n)").rearrange("p (t c) -> p t c", c=C)]
        xno = [aT.rearrange("p (t c) -> p t c", c=C),
               V[:, :, :, :].rearrange("p u b n -> p (u b n)").rearrange("p (t c) -> p t c", c=C)]
        xxb = [D[:, u, :].rearrange("p (c n) -> p c n", c=CC) for u in range(2)]
        xtok = w2[:, 0:NT * C].rearrange("p (n c) -> p n c", n=NT)
        lgT = [sq[0:E, :, :].rearrange("p b n -> p (b n)"), z[0:E, :, :].rearrange("p b n -> p (b n)")]
        lgs = hs[:, 0:NT * E]
        wA = tg[:, 0, :, :].rearrange("p r n -> p (r n)")[:, 0:CC * GR].rearrange("p (c n) -> p c n", c=CC)
        wrt = hs[:, 256:256 + CC * E].rearrange("p (c n) -> p c n", c=CC)
        hcode = [w1[LORA * k:LORA * (k + 1), 0:NS * 512] for k in range(2)]
        braw = mix[:, :, :, :, :].rearrange("p s c b n -> p (s c b n)")[:, 0:NS * C].rearrange("p (s n) -> p s n", s=NS)
        xdr = io["x"].rearrange("(b h t p) c -> b h p t c", b=NB, h=2, t=4)

        for dst, src in ((con[:, :], io["con"]), (vec[:, :], io["vec"]), (brc[:, :], io["br"]),
                         (wrt, io["Wr"].rearrange("(c p) n -> p c n", p=P))):
            done("q_c1", "c1", act.dma_start(dst, src))
        done("q_c1", "c1", act.dma_start(wA, io["A"].rearrange("(c p) n -> p c n", p=P)))
        for q in range(4):
            done("q_c2", "c2", act.dma_start(braw[LORA * q:LORA * (q + 1), :, :], io["Bp"].rearrange("s r c -> r s c")))
        done("q_c2", "c2", act.dma_start(rout, io["rout"]))

        mhalf = small[:, 59:60]
        done("pool", "mhalf", pool.memset(mhalf, -0.5))
        done("pool", "z_x0", pool.memset(xnT[:, :, :, 0:1], 0.0))
        done("pool", "z_hsT", pool.memset(hsT[:, :, :], 0.0))
        wait(pool, "mhalf")

        wait(dve, "z_x0")
        with nc.Fori(0, NB) as b:
            fl.enter("ln", NB, b)
            for hf in range(2):
                st = small[:, 0:24].rearrange("p (t s) -> p t s", t=4)
                mv = small[:, 24 + 12 * hf:32 + 12 * hf].rearrange("p (t s) -> p t s", t=4)
                rs = small[:, 32 + 12 * hf:36 + 12 * hf]
                wait(sp, (f"xn{hf}", 1))
                done(f"q_x{hf}", f"x{hf}", sp.dma_start(xin[hf], xdr[bass.ds(b, 1), hf, :, :, :]))
            for hf in range(2):
                st = small[:, 0:24].rearrange("p (t s) -> p t s", t=4)
                mv = small[:, 24 + 12 * hf:32 + 12 * hf].rearrange("p (t s) -> p t s", t=4)
                rs = small[:, 32 + 12 * hf:36 + 12 * hf]
                wait(dve, f"x{hf}")
                for t in range(4):
                    i1 = dve.bn_stats(st[:, t, :], xin[hf][:, t, :])
                done("dve", f"bn{hf}", i1)
                wait(dve, f"bn{hf}")
                settle(dve)
                for t in range(4):
                    i1 = dve.bn_aggr(mv[:, t, :], st[:, t, :])
                done("dve", f"ag{hf}", i1)
                wait(dve, f"ag{hf}")
                done("dve", f"ve{hf}", dve.tensor_scalar(rs, mv[:, :, 1], EPS_LN, None, ALU.add))
                wait(pool, f"ve{hf}")
                done("pool", f"rs{hf}", pool.tensor_tensor(rs, rs, mhalf[:, 0:1].broadcast_to([P, 4]), ALU.pow))
                wait(dve, f"rs{hf}", (f"tr{hf}", 1), (f"xt{hf}", 1))
                for t in range(4):
                    i1 = dve.tensor_scalar(xno[hf][:, t, :], xin[hf][:, t, :], mv[:, t, 0:1], rs[:, t:t + 1], ALU.subtract, ALU.mult)
                done("dve", f"xn{hf}", i1)
                wait(pool, f"xn{hf}")
                done("pool", f"xt{hf}", pool.tensor_copy(xtok[:, bass.ds(b * 8 + 4 * hf, 4), :], xno[hf]))
                bank = [G[0], G[1]] if hf == 0 else [FA, FB]
                wait(pe, f"xn{hf}", (f"h{hf}", 1), "c1")
                for cc in range(CC):
                    for t in range(4):
                        i1 = pe.transpose(bank[cc][:, P * t:P * (t + 1)], xno[hf][:, t, cc * P:(cc + 1) * P], ident)
                done("pe", f"tr{hf}", i1)
                wait(act, f"tr{hf}")
                span = slice(1 + 512 * hf, 1 + 512 * (hf + 1))
                for cc in range(CC):
                    i1 = act.activation(xnT[:, cc, bass.ds(b, 1), span].rearrange("p o n -> p (o n)"), bank[cc][:, :], ACT.Copy)
                done("act", f"tc{hf}", i1)
                wait(pe, f"tc{hf}", (f"lc{hf}", 1))
                for cc in range(CC):
                    i1 = pe.matmul(L[hf][0:E, :], wrt[:, cc, :], xnT[:, cc, bass.ds(b, 1), span].rearrange("p o n -> p (o n)"),
                                   start=(cc == 0), stop=(cc == CC - 1))
                done("pe", f"lg{hf}", i1)
                wait(act, f"lg{hf}", (f"lt{hf}", 1), "c1")
                done("act", f"lc{hf}", act.activation(lgT[hf], L[hf][0:E, :], ACT.Identity, bias=brc[:, 0:1]))
                span0 = slice(512 * hf, 512 * (hf + 1))
                xx = xxb[hf]
                xrow = xnT[:, :, bass.ds(b, 1), span].rearrange("p c o n -> p (c o) n")
                wait(dve, f"tc{hf}", (f"hm{hf}", 1))
                done("dve", f"xd{hf}", dve.tensor_tensor(xx, xnT[:, :, bass.ds(b, 1), span0].rearrange("p c o n -> p (c o) n"), xrow, ALU.subtract))
                wait(dve, f"xd{hf}")
                for cc in range(CC):
                    i1 = dve.scalar_tensor_tensor(xx[:, cc, :], xx[:, cc, :], cvec(MX, cc), xnT[:, cc, bass.ds(b, 1), span].rearrange("p o n -> p (o n)"), ALU.mult, ALU.add)
                done("dve", f"xx{hf}", i1)
                cb = [G[0], G[1]] if hf == 0 else [FA, FB]
                wait(pe, f"xx{hf}", f"tc{hf}")
                for cc in range(CC):
                    pe.matmul(cb[0][:, :], wA[:, cc, 0:P], xx[:, cc, :], start=(cc == 0), stop=(cc == 1))
                for cc in range(CC):
                    i1 = pe.matmul(cb[1][0:LORA, :], wA[:, cc, P:GR], xx[:, cc, :], start=(cc == 0), stop=(cc == 1))
                done("pe", f"hm{hf}", i1)
                wait(act, f"hm{hf}", (f"cs{hf}", 1))
                for g in range(NS):
                    src = cb[0][LORA * g:LORA * (g + 1), :] if g < 4 else cb[1][0:LORA, :]
                    i1 = act.activation(hcode[hf][:, g:NS * 511 + g + 1:NS], src, ACT.Tanh)
                done("act", f"h{hf}", i1)
                wait(sp, f"h{hf}")
                done(f"q_cs{hf}", f"cs{hf}", sp.dma_start(cd_d[:, bass.ds(b * (NS * T) + hf * (NS * 512), NS * 512)], hcode[hf]))
                lb = Y if hf == 0 else BB
                wait(pe, f"lc{hf}", (f"ls{hf}", 1))
                settle(pe)
                for t in range(4):
                    i1 = pe.transpose(lb[:, E * t:E * (t + 1)], lgT[hf][:, P * t:P * (t + 1)], con[0:E, IDN:IDN + E])
                done("pe", f"lt{hf}", i1)
                wait(act, f"lt{hf}")
                done("act", f"ls{hf}", act.activation(lgs[:, bass.ds((b * 8 + 4 * hf) * E, 4 * E)], lb[:, 0:4 * E], ACT.Copy))
            fl.leave()

        zsrc = hsT[:, :, :].rearrange("p h n -> p (h n)").rearrange("p (a c) -> p a c", c=C)
        wait(sp, "z_hsT")
        for n in range(0, FT, 2):
            a = min(2, FT - n)
            done("q_zero", "zero", sp.dma_start(xs_d[n * P:(n + a) * P, :].rearrange("(p a) c -> p a c", a=a), zsrc[:, 0:a, :]))
        pool.memset(S[:, :, :, :], 0.0)
        done("pool", "z_S", pool.memset(AP_[:, :, :, :, :], 0.0))
        done("q_zero", "zero", sp.dma_start(cd_d[:, CODES:CODES + P], zsrc[0:LORA, 0, 0:P]))
        for dst, src in (
                (tdA[:, :, :], io["tdA"].rearrange("(c p) n -> p c n", p=P)), (tdB[:, :], io["tdB"]),
                (wk[:, :, :], io["WkT"].rearrange("(c p) n -> p c n", p=P)),
                (wv[:, :, :], io["WvT"].rearrange("(c p) n -> p c n", p=P)),
                (wr[:, :, :], io["WrT"].rearrange("(c p) n -> p c n", p=P)),
                (wg1[:, :, :], io["Wg1"].rearrange("(c p) n -> p c n", p=P)),
                (wo[:, :, :], io["WoT"].rearrange("(c p) n -> p c n", p=P)),
                (wg2[:, 0, :], io["Wg2"][0:P, :]), (wg2[0:GR - P, 1, :], io["Wg2"][P:GR, :]),
                (gab[:, 0, :], io["gamma"].partition_broadcast(P)), (gab[:, 1, :], io["beta"].partition_broadcast(P)),
                (msk[:, :, :], io["msk"])):
            done("q_w", "w", sp.dma_start(dst, src))
        done("q_ew1", "ew1", sp.dma_start(b1c[:, :], io["b1c"]))
        wait(sp, "ln/cs0", "ln/cs1")
        for e in range(E):
            done("q_ew1", "ew1", sp.dma_start(w1[:, e * CC * HID:(e + 1) * CC * HID].rearrange("p (c n) -> p c n", c=CC),
                                              io["W1"][e].rearrange("(c p) n -> p c n", p=P)))

        wait(dve, "c2")
        done("dve", "bhi", dve.tensor_copy(bst[:, :, :], braw))
        wait(dve, "bhi")
        for q in (1, 3):
            i1 = dve.tensor_tensor(bst[LORA * q:LORA * (q + 1), :, :], braw[LORA * q:LORA * (q + 1), :, :],
                                   bst[LORA * q:LORA * (q + 1), :, :].bitcast(F32), ALU.subtract)
        done("dve", "bst", i1)
        mwv = small[:, 48:56]
        wv3 = wv[:, :, :].rearrange("p c (h i) -> p (c h) i", i=HEAD)
        wait(dve, "w")
        done("dve", "wv_s", dve.tensor_reduce(mwv, wv3, AX.X, ALU.add))
        wait(dve, "wv_s")
        done("dve", "wv_m", dve.tensor_scalar(mwv, mwv, 1.0 / HEAD, None, ALU.mult))
        wait(dve, "wv_m")
        done("dve", "wv_c", dve.tensor_tensor(wv3, wv3, mwv.rearrange("p (g o) -> p g o", o=1).broadcast_to([P, CC * GROUPS, HEAD]), ALU.subtract))

        def routing():
            def area(n):
                return res[:, n // 2, :, :].rearrange("p b c -> p (b c)")[:, 256 * (n % 2):256 * (n % 2) + 256].rearrange("p (t e) -> p t e", e=E)

            ex, oh, pre, tot = (area(n) for n in range(4))
            Lg = lgs.rearrange("p (t e) -> p t e", e=E)
            m1 = small[:, 0:NT]

            def bc(a):
                return a.rearrange("p (t o) -> p t o", o=1).broadcast_to([P, NT, E])

            def step(name, ins):
                done("dve", name, ins)
                wait(dve, name)

            wait(dve, "ln/ls1", "ln/xn1")
            step("r_max", dve.tensor_reduce(m1, Lg, AX.X, ALU.max))
            step("r_sub", dve.tensor_tensor(ex, Lg, bc(m1), ALU.subtract))
            wait(act, "r_sub")
            done("act", "r_exp", act.activation(ex, ex, ACT.Exp))
            yield 1
            wait(dve, "r_exp")
            step("r_sum", dve.tensor_reduce(m1, ex, AX.X, ALU.add))
            step("r_rec", dve.reciprocal(m1, m1))
            step("r_prb", dve.tensor_tensor(ex, ex, bc(m1), ALU.mult))
            yield 1
            step("r_pmx", dve.tensor_reduce(prob[:, :], ex, AX.X, ALU.max))
            step("r_eq", dve.tensor_tensor(oh, ex, bc(prob[:, :]), ALU.is_equal))
            wait(dve, "c2")
            rank8 = rout[:, RANK8:RANK8 + NT * E].rearrange("p (t e) -> p t e", e=E)
            step("r_rk", dve.tensor_tensor(oh, oh, rank8, ALU.mult))
            yield 1
            step("r_rm", dve.tensor_reduce(m1, oh, AX.X, ALU.max))
            step("r_oh", dve.tensor_tensor(oh, rank8, bc(m1), ALU.is_equal))
            wait(pe, "r_oh", "c2")
            ohf = oh.rearrange("p t e -> p (t e)")
            pe.matmul(FA[:, 0:NT * E], con[:, TRI:TRI + P], ohf, start=True, stop=True)
            done("pe", "r_mm", pe.matmul(FB[:, 0:NT * E], con[:, ONE:ONE + P], ohf, start=True, stop=True))
            yield 1
            wait(dve, "r_mm")
            dve.tensor_copy(pre, FA[:, 0:NT * E].rearrange("p (t e) -> p t e", e=E))
            step("r_tot", dve.tensor_copy(tot, FB[:, 0:NT * E].rearrange("p (t e) -> p t e", e=E)))
            for e in range(E):
                i1 = dve.tensor_tensor_scan(ex[:, :, e], tot[:, :, e], tot[:, :, e], 0.0, ALU.add, ALU.bypass)
            step("r_scan", i1)
            yield 1
            cnt = ex[:, NT - 1, :]
            tl = small[:, 32:40]
            en = small[:, 40:48]
            cmp = lgs.rearrange("p (e j) -> p e j", e=E)
            tile_at = rout[:, TILE_AT:TILE_AT + E * NT].rearrange("p (e j) -> p e j", e=E)
            step("r_cmp", dve.tensor_tensor(cmp, cnt.rearrange("p (e o) -> p e o", o=1).broadcast_to([P, E, NT]), tile_at, ALU.is_gt))
            step("r_tl", dve.tensor_reduce(tl, cmp, AX.X, ALU.add))
            step("r_en", dve.tensor_tensor_scan(en, tl, tl, 0.0, ALU.add, ALU.bypass))
            step("r_s0", dve.tensor_tensor(tl, en, tl, ALU.subtract))
            step("r_s1", dve.tensor_scalar(tl, tl, float(P), None, ALU.mult))
            yield 1
            step("r_s2", dve.tensor_tensor(pre, pre, ex, ALU.add))
            step("r_s3", dve.tensor_tensor(pre, pre, tot, ALU.subtract))
            step("r_s4", dve.tensor_tensor(pre, pre, tl.rearrange("p (o e) -> p o e", o=1).broadcast_to([P, NT, E]), ALU.add))
            yield 1
            step("r_s5", dve.tensor_tensor(pre, pre, oh, ALU.mult))
            step("r_s6", dve.tensor_reduce(m1, pre, AX.X, ALU.add))
            done("dve", "r_slot", dve.tensor_copy(slot[:, :], m1))
            wait(pool, "r_slot", "zero", "ln/xt0", "ln/xt1")
            for t in range(NT):
                done("q_scat", "scat", pool.indirect_dma_start(xs_d, bass.IndirectOffsetOnAxis(slot[:, t:t + 1], 0), xtok[:, t, :], None))
            yield 1
            tno = rout[0:1, TILE_NO:TILE_NO + FT * (E - 1)].rearrange("p (j e) -> p j e", e=E - 1)
            w2c = res[0:1, 1, :, :].rearrange("p b c -> p (b c)")[:, 0:FT * (E - 1)].rearrange("p (j e) -> p j e", e=E - 1)
            ef = small[0:1, 0:FT]
            step("r_c2", dve.tensor_tensor(w2c, tno, en[0:1, 0:E - 1].rearrange("p (o e) -> p o e", o=1).broadcast_to([1, FT, E - 1]), ALU.is_ge))
            step("r_ef", dve.tensor_reduce(ef, w2c, AX.X, ALU.add))
            step("r_ex", dve.tensor_copy(expert[:, :], ef))
            wait(sp, "scat")
            for e in range(E):
                done("q_ew2", "ew2", sp.dma_start(w2[:, e * HC * C:(e + 1) * HC * C].rearrange("p (c n) -> p c n", c=HC),
                                                  io["W2"][e].rearrange("(c p) n -> p c n", p=P)))
            yield 1

        fl.stream = "front"
        xres = io["x"].rearrange("(u b k p) c -> k u p b c", u=2, b=UB, k=NCH)
        aout = at_d.rearrange("(u b k p) c -> k u p b c", u=2, b=UB, k=NCH)

        def codes(u, c):
            first = fl.place == "once"
            if not first:
                wait(sp, "clo.1" if u == 0 else "once/clo.0" if fl.place == "pre" else ("clo.0", 1))
            src = cd_d[:, bass.ds(c * P, CODES)].rearrange("r (s b t) -> r s b t", s=NS, b=NB)
            for q in range(4):
                for b in range(UB):
                    done("q_cr", f"cr.{u}", sp.dma_start(craw[LORA * q:LORA * (q + 1), :, b * P:(b + 1) * P], src[:, :, UB * u + b, 0:P]))
            yield 0.0
            wait(act, f"cr.{u}", *([] if first else [(f"mm4.{u}", 1 if u else 0)]))
            done("act", f"chi.{u}", act.activation(cd[:, u, :, :], craw[:, :, :], ACT.Copy))
            yield 0.0
            wait(dve, f"chi.{u}")
            done("dve", f"clo.{u}", dve.tensor_tensor(cd[P // 2:P, u, :, :], craw[P // 2:P, :, :], cd[P // 2:P, u, :, :].bitcast(F32), ALU.subtract))
            yield 0.0

        CHUNK_TOT = sum(CC * UN // B for B in (1, 2, 4, 8, 16, 32, 64))

        def fl2(a):
            return a.rearrange("p c b n -> p (c b n)")

        FRONT_USES = ("m0", "m1", "tw", "m2", "d", "k", "m3", "v", "m4", "r", "tg")

        def front(u, c):
            o = 1 - u
            pre = fl.place == "pre"
            other = lambda name: (f"{name}.{o}", 1 if u == 0 else 0)
            pairs_ = lambda name: (f"{name}.{u}", 1 if u == 0 or pre else 0)
            tail_ = lambda name: (f"{name}.{u}", 1 if pre else 0)
            uses = []
            if not (pre and u == 0):
                wait(pe, ("clo.0", 1) if u == 0 else "clo.1")

            def bank(name):
                n = len(uses)
                assert FRONT_USES[n] == name
                uses.append(name)
                wait(pe, f"{FRONT_USES[n - 2]}.{u}" if n > 1 else other(FRONT_USES[n - 2]))
                return G[(n + u) % 2]

            xc = xnT[:, :, UB * u:UB * (u + 1), bass.ds(c * P + 1, P)]
            xp = xnT[:, :, UB * u:UB * (u + 1), bass.ds(c * P, P)]
            wait(pool, other("m4"))
            settle(pool)
            done("pool", f"ba.{u}", pool.tensor_tensor(ba[:, :, :, :], xp, xc, ALU.subtract))
            readers = {0: other("rm"), 1: other("gm"), 2: other("vm"), 3: f"tA.{u}", 4: f"km.{u}"}

            def mixed(s):
                bk = bank(f"m{s}")
                for cc in range(CC):
                    i1 = pe.matmul(bk[:, cc * UN:(cc + 1) * UN], bst[:, s, cc * P:(cc + 1) * P], cd[:, u, s, :], start=True, stop=True)
                done("pe", f"mm{s}.{u}", i1)
                buf = mix[:, s % 3, :, :, :]
                wait(dve, f"mm{s}.{u}", f"ba.{u}", readers[s])
                for cc in range(CC):
                    i1 = dve.scalar_tensor_tensor(
                        buf[:, cc, :, :].rearrange("p b n -> p (b n)"), bk[:, cc * UN:(cc + 1) * UN],
                        vec[:, LAM + CC * s + cc:LAM + CC * s + cc + 1], ba[:, cc, :, :].rearrange("p b n -> p (b n)"), ALU.add, ALU.mult)
                done("dve", f"m{s}.{u}", i1)
                wait(pool, f"m{s}.{u}")
                settle(pool)
                done("pool", f"x{s}.{u}", pool.tensor_tensor(buf, buf, xc, ALU.add))

            def src(s, cc):
                return mix[:, s % 3, cc, :, :].rearrange("p b n -> p (b n)")

            mixed(0)
            yield 0.25
            mixed(1)
            yield 0.25
            bk = bank("tw")
            wait(pe, f"x0.{u}")
            for cc in range(CC):
                i1 = pe.matmul(bk[0:TDR, 0:UN], tdA[:, cc, :], src(0, cc), start=(cc == 0), stop=(cc == 1))
            done("pe", f"tA.{u}", i1)
            wait(act, f"tA.{u}", other("tB"))
            done("act", f"tw.{u}", act.activation(tw[:, :], bk[0:TDR, 0:UN], ACT.Tanh))
            yield 0.25
            mixed(2)
            yield 0.25
            bk = bank("d")
            wait(pe, f"tw.{u}")
            for cc in range(CC):
                i1 = pe.matmul(bk[:, cc * UN:(cc + 1) * UN], tdB[:, cc * P:(cc + 1) * P], tw[:, :], start=True, stop=True)
            done("pe", f"tB.{u}", i1)
            wait(act, f"tB.{u}", pairs_("gr1"))
            for cc in range(CC):
                i1 = act.activation(D[:, u, cc * UN:(cc + 1) * UN], bk[:, cc * UN:(cc + 1) * UN], ACT.Exp, bias=cvec(TDM, cc))
            done("act", f"d.{u}", i1)
            yield 0.9

            def project(w, s, bk):
                for co in range(CC):
                    for cc in range(CC):
                        i1 = pe.matmul(bk[:, co * UN:(co + 1) * UN], w[:, cc, co * P:(co + 1) * P], src(s, cc), start=(cc == 0), stop=(cc == 1))
                return i1

            bk = bank("k")
            wait(pe, f"x1.{u}")
            done("pe", f"km.{u}", project(wk, 1, bk))
            wait(dve, f"km.{u}", f"d.{u}", tail_("kT"))
            done("dve", f"k.{u}", dve.scalar_tensor_tensor(fl2(K[:, u]), D[:, u, 0:CC * UN], 1.0, bk[:, :], ALU.min, ALU.mult))
            yield 1.7
            mixed(3)
            yield 0.25
            bk = bank("v")
            wait(pe, f"x2.{u}")
            for b in range(UB):
                for cc in range(CC):
                    i1 = pe.matmul(bk[:, b * C:(b + 1) * C], mix[:, 2, cc, b, :], wv[:, cc, :], start=(cc == 0), stop=(cc == 1))
            done("pe", f"vm.{u}", i1)
            wait(act, f"vm.{u}", tail_("sm"))
            done("act", f"v.{u}", act.activation(V[:, u, :, :].rearrange("p b n -> p (b n)"), bk[:, :], ACT.Copy))
            yield 1.7
            mixed(4)
            yield 0.25
            bk = bank("r")
            wait(pe, f"x3.{u}")
            done("pe", f"rm.{u}", project(wr, 3, bk))
            wait(act, f"rm.{u}", tail_("y"))
            done("act", f"r.{u}", act.activation(fl2(R[:, u]), bk[:, :], ACT.Copy))
            yield 1.7
            bk = bank("tg")
            wait(pe, f"x4.{u}")
            for k, (m0, m1_) in enumerate(((0, P), (P, GR))):
                for cc in range(CC):
                    i1 = pe.matmul(bk[0:m1_ - m0, k * UN:(k + 1) * UN], wg1[:, cc, m0:m1_], src(4, cc), start=(cc == 0), stop=(cc == 1))
            done("pe", f"gm.{u}", i1)
            wait(act, f"gm.{u}", tail_("gg"))
            for k, rows in enumerate((P, GR - P)):
                i1 = act.activation(tg[0:rows, u, k, :], bk[0:rows, k * UN:(k + 1) * UN], ACT.Tanh)
            done("act", f"tg.{u}", i1)
            yield 1.7

        def pairs(u, c):
            lag = 1 if u == 1 else 0
            o = 1 - u
            pre = fl.place == "pre"
            F = lambda name: (f"{name}.{u}", lag)
            before = lambda name: (f"{name}.{o}", 1 if u == 1 or pre else 0)
            tail_ = lambda name: (f"{name}.{u}", 1 if u == 1 or pre else 0)
            Ku_, Ru, Du = K[:, u], R[:, u], D[:, u, :]
            cols = CC * UN

            wait(act, F("k"), before("l01"))
            for cc in range(CC):
                i1 = act.activation(Ku[:, cc, :, :].rearrange("p b n -> p (b n)"), K[:, u, cc, :, :].rearrange("p b n -> p (b n)"),
                                    ACT.Copy, scale=cvec(UU, cc))
            done("act", f"ku.{u}", i1)
            yield 0.0

            def tots(B):
                at = 0 if B == 1 else sum(cols // b for b in (1, 2, 4, 8, 16, 32, 64) if b < B)
                return Du[:, at:at + cols // B]

            def grow(B):
                n = cols // (2 * B)
                half = lambda a: fl2(a).rearrange("p (n h t) -> p n h t", h=2, t=B)
                tt = tots(B).rearrange("p (n h) -> p n h", h=2)
                wide = lambda a: a.rearrange("p (n o) -> p n o", o=1).broadcast_to([P, n, B])
                r2, k2 = half(Ru)[:, :, 1, :], half(Ku_)[:, :, 0, :]
                dve.tensor_tensor(r2, r2, wide(tt[:, :, 0]), ALU.mult)
                dve.tensor_tensor(k2, k2, wide(tt[:, :, 1]), ALU.mult)
                done("dve", f"gr{B}.{u}", dve.tensor_tensor(tots(2 * B), tt[:, :, 0], tt[:, :, 1], ALU.mult))

            for li, B in enumerate(LEVELS):
                if li == 0:
                    wait(pe, f"ku.{u}", F("r"))
                elif B > 1:
                    wait(pe, f"gr{B // 2}.{u}")
                Ks = Ku if li == 0 else Ku_
                for h in range(H2):
                    wait(pe, *([before(f"e64{h}")] if li == 0 else [f"a{li - 1}{h}.{u}"]))
                    settle(pe)
                    rows = slice(HEAD * h, HEAD * (h + 1))
                    for cc in range(CC):
                        for b in range(UB):
                            for q in range(P // LEAF):
                                i1 = pe.matmul(L[h][LEAF * q:LEAF * (q + 1), (cc * UB + b) * LEAF:(cc * UB + b + 1) * LEAF],
                                               Ks[rows, cc, b, LEAF * q:LEAF * (q + 1)], Ru[rows, cc, b, LEAF * q:LEAF * (q + 1)],
                                               start=True, stop=True, tile_position=(HEAD * h, LEAF * q))
                    done("pe", f"l{li}{h}.{u}", i1)
                    wait(dve, f"l{li}{h}.{u}", *([before("spread")] if li == 0 else [f"a{li - 1}{h}.{u}"]))
                    settle(dve)
                    m = msk[:, li:li + 1, :].broadcast_to([P, CC * UB, LEAF])
                    done("dve", f"a{li}{h}.{u}", dve.copy_predicated(
                        AP_[:, h, :, :, :].rearrange("p c b n -> p (c b) n"), m,
                        L[h][:, 0:CC * UB * LEAF].rearrange("p (g n) -> p g n", n=LEAF)))
                    if h == 0:
                        yield 0.7
                if B >= 1:
                    wait(dve, F("d") if B == 1 else f"gr{B // 2}.{u}")
                    grow(B)
                yield 0.7
            for B in (32, 64):
                wait(pe, f"gr{B // 2}.{u}")
                for h in range(H2):
                    wait(pe, f"a{len(LEVELS) - 1}{h}.{u}" if B == 32 else f"e32{h}.{u}")
                    settle(pe)
                    rows = slice(HEAD * h, HEAD * (h + 1))
                    for cc in range(CC):
                        for b in range(UB):
                            for s0 in range(0, P, 2 * B):
                                i1 = pe.matmul(L[h][s0:s0 + B, (cc * UB + b) * B:(cc * UB + b + 1) * B], Ku_[rows, cc, b, s0:s0 + B],
                                               Ru[rows, cc, b, s0 + B:s0 + 2 * B], start=True, stop=True, tile_position=(HEAD * h, s0))
                    done("pe", f"l{B}{h}.{u}", i1)
                    wait(act, f"l{B}{h}.{u}", tail_("y"))
                    for s0 in range(0, P, 2 * B):
                        i1 = act.activation(AT[s0:s0 + B, u, h, :, :, s0 + B:s0 + 2 * B].rearrange("p c b n -> p (c b) n"),
                                            L[h][s0:s0 + B, 0:CC * UB * B].rearrange("p (g n) -> p g n", n=B), ACT.Copy)
                    done("act", f"e{B}{h}.{u}", i1)
                    if h == 0:
                        yield 0.5
                wait(dve, f"gr{B // 2}.{u}", f"l{B}1.{u}", *([tail_("S_dec")] if B == 64 else []))
                grow(B)
                yield 0.5
            wait(act, *[f"a{len(LEVELS) - 1}{h}.{u}" for h in range(H2)])
            for q in range(P // LEAF):
                i1 = act.activation(AT[LEAF * q:LEAF * (q + 1), u, :, :, :, LEAF * q:LEAF * (q + 1)].rearrange("p h c b n -> p (h c b) n"),
                                    AP_[LEAF * q:LEAF * (q + 1), :, :, :, :].rearrange("p h c b n -> p (h c b) n"), ACT.Copy)
            done("act", f"spread.{u}", i1)

            yield 0.0

        def tail(u, c):
            o = 1 - u
            F = lambda name: (f"{name}.{u}", 1)
            pairs_ = lambda name: (f"{name}.{u}", 1 if u == 0 else 0)
            before = lambda name: (f"{name}.{o}", 1 if u == 0 else 0)
            Ru = R[:, u]
            tot = D[:, u, :][:, CHUNK_TOT:CHUNK_TOT + CC * UB]
            flat = lambda a: a[:, :, :].rearrange("p b n -> p (b n)")

            wait(sp, (f"st.{u}", 1))
            done(f"q_res{u}", f"res.{u}", sp.dma_start(res[:, u, :, :], xres[bass.ds(c, 1), u, :, :, :].rearrange("o p b c -> p (o b) c")))

            wait(pe, pairs_("gr64"), before("o"))
            for b in range(UB):
                for cc in range(CC):
                    i1 = pe.transpose(BB[:, b * C + cc * P:b * C + (cc + 1) * P], K[:, u, cc, b, :], ident)
            done("pe", f"kT.{u}", i1)
            yield 0.45
            wait(act, f"kT.{u}", before("z"))
            done("act", f"kt.{u}", act.activation(flat(Kt), BB[:, :], ACT.Copy))

            wait(pe, pairs_("spread"), F("v"), (f"S_new.{u}", 1), before("zc"))
            settle(pe)
            for b in range(UB):
                for cc in range(CC):
                    at = b * C + cc * P
                    pe.matmul(Y[:, at:at + P], Ru[:, cc, b, :], S[:, u, b * CC + cc, :], start=True, stop=False)
                    for h in range(H2):
                        i1 = pe.matmul(Y[:, at + HEAD * h:at + HEAD * (h + 1)], AT[:, u, h, cc, b, :],
                                       V[:, u, b, cc * P + h * HEAD:cc * P + (h + 1) * HEAD], start=False, stop=(h == H2 - 1))
                if b == 0:
                    yield 1.3
            done("pe", f"y.{u}", i1)
            wait(act, f"y.{u}", before("om"))
            done("act", f"sq.{u}", act.activation(flat(sq), Y[:, :], ACT.Square))
            wait(dve, f"y.{u}", pairs_("gr64"))
            for h in range(H2):
                Sh = S[HEAD * h:HEAD * (h + 1), u, :, HEAD * h:HEAD * (h + 1)].rearrange("p (b c) i -> p c b i", b=UB)
                for cc in range(CC):
                    i1 = dve.tensor_tensor(Sh[:, cc], Sh[:, cc], tot[HEAD * h:HEAD * (h + 1), cc * UB:(cc + 1) * UB]
                                           .rearrange("p (b o) -> p b o", o=1).broadcast_to([HEAD, UB, HEAD]), ALU.mult)
            done("dve", f"S_dec.{u}", i1)
            yield 1.3
            wait(pe, f"kt.{u}")
            settle(pe)
            for b in range(UB):
                for cc in range(CC):
                    for h in range(H2):
                        g = b * CC + cc
                        i1 = pe.matmul(BB[HEAD * h:HEAD * (h + 1), g * HEAD:(g + 1) * HEAD],
                                       Kt[:, b, cc * P + HEAD * h:cc * P + HEAD * (h + 1)], V[:, u, b, cc * P + h * HEAD:cc * P + (h + 1) * HEAD],
                                       start=True, stop=True, tile_position=(0, HEAD * h))
            done("pe", f"sm.{u}", i1)
            wait(dve, f"sm.{u}", f"S_dec.{u}")
            for h in range(H2):
                Sh = S[HEAD * h:HEAD * (h + 1), u, :, HEAD * h:HEAD * (h + 1)]
                i1 = dve.tensor_tensor(Sh, Sh, BB[HEAD * h:HEAD * (h + 1), 0:UB * CC * HEAD].rearrange("p (g i) -> p g i", i=HEAD), ALU.add)
            done("dve", f"S_new.{u}", i1)
            yield 0.9

            wait(pe, F("tg"), f"S_new.{u}")
            for b in range(UB):
                o_ = BB[:, b * C:(b + 1) * C]
                pe.matmul(o_, tg[:, u, 0, b * P:(b + 1) * P], wg2[:, 0, :], start=True, stop=False)
                i1 = pe.matmul(o_, tg[0:GR - P, u, 1, b * P:(b + 1) * P], wg2[0:GR - P, 1, :], start=False, stop=True)
            done("pe", f"gg.{u}", i1)
            yield 1.7
            heads = lambda a: a.rearrange("p (g i) -> p g i", i=HEAD)
            wait(dve, f"sq.{u}")
            done("dve", f"va.{u}", dve.tensor_reduce(gv, heads(flat(sq)), AX.X, ALU.add))
            wait(dve, f"va.{u}")
            done("dve", f"gv.{u}", dve.tensor_scalar(gv, gv, 1.0 / HEAD, EPS_GN, ALU.mult, ALU.add))
            wait(pool, f"gv.{u}")
            done("pool", f"gy.{u}", pool.tensor_tensor(gy, gv, mhalf[:, 0:1].broadcast_to([P, UB * GROUPS]), ALU.pow))
            yield 0.0
            wait(dve, f"gy.{u}", f"sm.{u}")
            done("dve", f"yg.{u}", dve.tensor_tensor(heads(flat(yn)), heads(Y[:, :]), gy.rearrange("p (g o) -> p g o", o=1).broadcast_to([P, UB * GROUPS, HEAD]), ALU.mult))
            both = lambda n: gab[:, n:n + 1, :].broadcast_to([P, UB, C])
            wait(pool, f"yg.{u}")
            done("pool", f"ym.{u}", pool.tensor_tensor(yn[:, :, :], yn[:, :, :], both(0), ALU.mult))
            wait(pool, f"ym.{u}")
            done("pool", f"yb.{u}", pool.tensor_tensor(yn[:, :, :], yn[:, :, :], both(1), ALU.add))
            yield 0.0
            wait(dve, f"gg.{u}", f"yb.{u}")
            done("dve", f"z.{u}", dve.tensor_tensor(flat(z), flat(yn), BB[:, :], ALU.mult))
            yield 0.0
            wait(pe, f"z.{u}")
            for b in range(UB):
                for cc in range(CC):
                    i1 = pe.transpose(Y[:, b * C + cc * P:b * C + (cc + 1) * P], z[:, b, cc * P:(cc + 1) * P], ident)
            done("pe", f"zt.{u}", i1)
            wait(act, f"zt.{u}")
            done("act", f"zc.{u}", act.activation(flat(zT), Y[:, :], ACT.Copy))
            yield 0.45
            wait(pe, f"zc.{u}")
            for b in range(UB):
                for cc in range(CC):
                    i1 = pe.matmul(BB[:, b * C:(b + 1) * C], zT[:, b, cc * P:(cc + 1) * P], wo[:, cc, :], start=(cc == 0), stop=(cc == 1))
            done("pe", f"om.{u}", i1)
            wait(dve, f"om.{u}", f"res.{u}")
            r2 = res[:, u, :, :].rearrange("p b n -> p (b n)")
            done("dve", f"o.{u}", dve.tensor_tensor(r2, r2, BB[:, :], ALU.add))
            wait(sp, f"o.{u}")
            done(f"q_st{u}", f"st.{u}", sp.dma_start(aout[bass.ds(c, 1), u, :, :, :].rearrange("o p b c -> p (o b) c"), res[:, u, :, :]))
            yield 1.7

        def experts(first, tiles):
            for f in range(tiles):
                was = (lambda n: (f"{n}{FPI - 1}", 1)) if f == 0 else (lambda n: f"{n}{f - 1}")
                ahead = ([0] if f == 0 else []) + ([f + 1] if f + 1 < tiles else [])
                for g in ahead:
                    k = g % 2
                    user = g - 2 if g > 1 else max(n for n in range(FPI) if n % 2 == k)
                    lag = 0 if g > 1 else 1
                    wait(sp, (f"fxt{user}", lag), (f"fy{user}", lag))
                    done(f"q_xs{k}", f"xs{g}", sp.dma_start(xs[:, k, :], xs_d[bass.ds(first * P + g * P, P), :]))
                    sv = sp.value_load(expert[0:1, bass.ds(first + g, 1)], min_val=0, max_val=E - 1)
                    done(f"q_b2{k}", f"b2{g}", sp.dma_start(b2t[:, k, :], io["b2"][bass.ds(sv * C, C)].partition_broadcast(P)))
                wait(pe, f"xs{f}", was("fh"))
                for cc in range(CC):
                    i1 = pe.transpose(FA[:, cc * P:(cc + 1) * P], xs[:, f % 2, cc * P:(cc + 1) * P], ident)
                done("pe", f"fxt{f}", i1)
                wait(act, f"fxt{f}", was("fhm"))
                done("act", f"fx{f}", act.activation(xsT[:, :, :].rearrange("p c n -> p (c n)"), FA[:, 0:C], ACT.Copy))
                ev = pe.value_load(expert[0:1, bass.ds(first + f, 1)], min_val=0, max_val=E - 1)
                av = act.value_load(expert[0:1, bass.ds(first + f, 1)], min_val=0, max_val=E - 1)
                yield 0.5
                wait(pe, f"fx{f}", was("fy"), "ew1")
                for cc in range(CC):
                    i1 = pe.matmul(FB[:, :], xsT[:, cc, :], w1[:, bass.ds(ev * (CC * HID) + cc * HID, HID)], start=(cc == 0), stop=(cc == 1))
                done("pe", f"fhm{f}", i1)
                yield 1.7
                wait(act, f"fhm{f}", was("fht"))
                done("act", f"fhc{f}", act.activation(hs[:, :], FB[:, :], ACT.Copy))
                yield 0.0
                wait(pe, f"fhc{f}")
                for k in range(HC):
                    i1 = pe.transpose(FA[:, k * P:(k + 1) * P], hs[:, k * P:(k + 1) * P], ident)
                done("pe", f"fht{f}", i1)
                yield 0.5
                wait(act, f"fht{f}", was("fym"))
                for k in range(HC):
                    i1 = act.activation(hsT[:, k, :], FA[:, k * P:(k + 1) * P], ACT.Relu, bias=b1c[:, bass.ds(av * HC + k, 1)])
                done("act", f"fh{f}", i1)
                yield 0.0
                wait(pe, f"fh{f}", "ew2")
                for k in range(HC):
                    i1 = pe.matmul(FB[:, 0:C], hsT[:, k, :], w2[:, bass.ds(ev * (HC * C) + k * C, C)], start=(k == 0), stop=(k == HC - 1))
                done("pe", f"fym{f}", i1)
                yield 1.7
                wait(dve, f"fym{f}", f"b2{f}", was("ys"))
                done("dve", f"fy{f}", dve.tensor_tensor(ys[:, :], FB[:, 0:C], b2t[:, f % 2, :], ALU.add))
                wait(sp, f"fy{f}")
                done("q_ys", f"ys{f}", sp.dma_start(ys_d[bass.ds(first * P + f * P, P), :], ys[:, :]))

        def chain(*parts):
            for part in parts:
                yield from part

        for e in (pe, dve, act, pool):
            wait(e, "ln/h0", "ln/h1", "ln/hm0", "ln/hm1", "ln/xx0", "ln/xx1", "ln/xt0", "ln/xt1", "ln/cs0", "ln/cs1",
                 "ln/lt0", "ln/lt1", "ln/lc0", "ln/lc1", "wv_c", "bst", "w")
        wait(sp, "zero")
        wait(act, "bst")
        done("pool", "z_AT0", pool.memset(aT, 0.0))
        for e in (pe, dve, act):
            wait(e, "z_S", "z_AT0")
        fl.stream = "codes"
        for _ in codes(0, 0):
            pass
        wait(pe, "clo.0")

        fl.enter("pre")
        interleave("a", ("front", chain(front(0, 0), front(1, 0))), ("pairs", pairs(0, 0)), ("route", routing()),
                   ("codes", chain(codes(1, 0), codes(0, 1))))
        fl.leave()
        fl.stream = "setup"
        wait(pool, "pre/r_ex")
        done("pool", "z_AT1", pool.memset(aT1, 0.0))
        for e in (pe, dve, act, sp):
            wait(e, "z_AT1", "pre/r_ex")
        with nc.Fori(0, TURNS) as c:
            fl.enter("main", TURNS, c)
            interleave("a", ("pairs", chain(pairs(1, c), pairs(0, c + 1))), ("tail", chain(tail(0, c), tail(1, c))),
                       ("front", chain(front(0, c + 1), front(1, c + 1))), ("experts", experts(c * FPI, FPI)),
                       ("codes", chain(codes(1, c + 1), codes(0, c + 2))))
            fl.leave()
        fl.enter("last")
        interleave("a", ("pairs", pairs(1, NCH - 1)), ("tail", chain(tail(0, NCH - 1), tail(1, NCH - 1))),
                   ("experts", experts(TURNS * FPI, FT - TURNS * FPI)))
        fl.leave()

        fl.stream = "end"
        adr = at_d.rearrange("(n t p) c -> n p t c", t=4, p=P)
        odr = io["out"].rearrange("(n t p) c -> n p t c", t=4, p=P)
        LASTF = FT - TURNS * FPI - 1
        as4 = lambda a: a.rearrange("p u b n -> p (u b n)").rearrange("p (t c) -> p t c", c=C)
        fa = [as4(res[:, :, :, :]), as4(V[:, :, :, :])]
        fg = [aT.rearrange("p (t c) -> p t c", c=C), R[:, :, :, :, :].rearrange("p u c b n -> p (u c b n)").rearrange("p (t c) -> p t c", c=C)]
        ix = small[:, 0:8].bitcast(I32)
        wait(sp, "last/st.0", "last/st.1", "last/sm.1", f"last/ys{LASTF}")
        wait(pool, "last/y.1", f"last/ys{LASTF}")
        with nc.Fori(0, NT // 8) as n:
            fl.enter("end", NT // 8, n)
            for k in range(2):
                wait(sp, (f"out{k}", 1))
                done(f"q_fa{k}", f"fa{k}", sp.dma_start(fa[k], adr[bass.ds(n * 2 + k, 1), :, :, :]))
                wait(pool, (f"fin{k}", 1))
                done("pool", f"ix{k}", pool.tensor_copy(ix[:, 4 * k:4 * k + 4], slot[:, bass.ds(n * 8 + 4 * k, 4)]))
                wait(pool, f"ix{k}")
                settle(pool)
                for t in range(4):
                    done(f"q_fg{k}", f"fg{k}", pool.indirect_dma_start(fg[k][:, t, :], None, ys_d, bass.IndirectOffsetOnAxis(ix[:, 4 * k + t:4 * k + t + 1], 0)))
                wait(dve, f"fa{k}", f"fg{k}")
                for t in range(4):
                    i1 = dve.scalar_tensor_tensor(fa[k][:, t, :], fg[k][:, t, :], prob[:, bass.ds(n * 8 + 4 * k + t, 1)], fa[k][:, t, :], ALU.mult, ALU.add)
                done("dve", f"fin{k}", i1)
            for k in range(2):
                wait(sp, f"fin{k}")
                done(f"q_out{k}", f"out{k}", sp.dma_start(odr[bass.ds(n * 2 + k, 1), :, :, :], fa[k]))
            fl.leave()
        wait(sp, "end/out0", "end/out1")
        return fl.summary()


def constants():
    con = np.zeros((P, NCONST), np.float32)
    con[:, IDN:IDN + P] = np.eye(P)
    a = np.arange(P)
    rout = np.zeros((P, NROUTE), np.float32)
    con[:, TRI:TRI + P] = a[:, None] < a[None]
    con[:, ONE:ONE + P] = 1
    rout[:, RANK8:RANK8 + NT * E] = np.tile(E - np.arange(E), NT)
    rout[:, TILE_AT:TILE_AT + E * NT] = np.tile(P * np.arange(NT), E)
    rout[:, TILE_NO:] = np.repeat(np.arange(FT), E - 1)
    msk = np.zeros((P, len(LEVELS), LEAF), np.uint32)
    s, t = (a % LEAF)[:, None], np.arange(LEAF)[None]
    for n, B in enumerate(LEVELS):
        msk[:, n] = (s == t) if B == 0 else (s // (2 * B) == t // (2 * B)) & (s % (2 * B) < B) & (t % (2 * B) >= B)
    return con, rout, msk


def kernel(**inp):
    import concourse.bacc as _bacc
    from concourse.bass_utils import run_bass_kernel_spmd as _run

    g = {k.replace("L0_attn_", "a_").replace("L0_ffn_", "f_"): np.asarray(v) for k, v in inp.items()}
    con, rout, msk = constants()
    col = lambda v: v.reshape(-1, CC, P).transpose(2, 0, 1).reshape(P, -1)
    vec = np.concatenate([col(g[n]) for n in ("a_miu_x", "a_td_miu", "a_u", "a_lam")], axis=1)
    arrays = {
        "x": g["a_x"].reshape(TOK, C), "con": con, "rout": rout, "msk": msk, "vec": vec,
        "gamma": g["a_gamma"].reshape(C), "beta": g["a_beta"].reshape(C),
        "A": g["a_A"], "Bp": g["a_Bp"], "tdA": g["a_tdA"], "tdB": g["a_tdB"],
        "WkT": g["a_Wk"].T, "WvT": g["a_Wv"].T, "WrT": g["a_Wr"].T, "WoT": g["a_Wo"].T,
        "Wg1": g["a_Wg1"], "Wg2": g["a_Wg2"], "Wr": g["f_Wr"], "br": g["f_br"].reshape(E, 1),
        "W1": g["f_W1"], "W2": g["f_W2"], "b1c": g["f_b1"].reshape(E * HC, P).T, "b2": g["f_b2"].reshape(E * C),
    }
    arrays = {k: np.ascontiguousarray(v) for k, v in arrays.items()}

    known = None
    for _ in range(2):
        nc = _bacc.Bacc("TRN2", target_bir_lowering=False, num_devices=1)
        io = {k: nc.dram_tensor(f"in_{k}", v.shape, mybir.dt.from_np(v.dtype), kind="ExternalInput").ap()
              for k, v in arrays.items()}
        io["out"] = nc.dram_tensor("out", (TOK, C), F32, kind="ExternalOutput").ap()
        known = program(nc, io, known)
    r = _run(nc, [{f"in_{k}": v for k, v in arrays.items()}], core_ids=[0])
    return r.results[0]["out"].reshape(NB, T, C)
```

```python
from contextlib import ExitStack

import numpy as np
import concourse.bass as bass
from concourse import mybir

F32 = mybir.dt.float32
F32R = mybir.dt.float32r
I32 = mybir.dt.int32
U32 = mybir.dt.uint32
ALU = mybir.AluOpType
ACT = mybir.ActivationFunctionType
AX = mybir.AxisListType

P = 128
NB, T, C = 4, 1024, 256
TOK = NB * T
CC = C // P
HEAD = 64
H2 = P // HEAD
NT = TOK // P
NCH = T // P
HID, E = 512, 8
HC = HID // P
LORA, NS = 32, 5
GR = NS * LORA
TDR = 64
GROUPS = CC * H2
EPS_LN = 1e-5
EPS_GN = 1e-5 * GROUPS
LEAF = 32
LEVELS = [0, 1, 2, 4, 8, 16]
UB = NB // 2
UN = UB * P
TURNS = NCH - 1
FT = (TOK + E * (P - 1)) // P
ZT = -(-FT // NB) + (-(-FT // NB)) % 2
FPI = FT // TURNS

COST = {"ku": 0.95, "chi": 1.2, "clo": 1.4, "d": 1.1, "tg": 0.6, "tw": 0.3, "spread": 1.2, "ym": 1.3, "yb": 1.3,
        "gr1": 0.9, "gr2": 0.9, "gr4": 0.8, "gr8": 0.7, "gr16": 0.7, "gr32": 0.7, "gr64": 0.7, "S_dec": 0.8,
        "ba": 1.2, "gy": 0.8, "cr": 4.0, "res": 2.5,
        **{f"m{s}": 0.8 for s in range(NS)}, **{f"x{s}": 1.2 for s in range(NS)},
        **{f"{n}{hf}": t for hf in (0, 1) for n, t in (("bn", 1.3), ("xn", 1.3), ("xd", 1.2), ("xx", 1.3), ("tc", 1.0), ("h", 2.4), ("xt", 3.6))},
        **{f"xs{f}": 2.5 for f in range(FPI)}, **{f"b2{f}": 2.5 for f in range(FPI)}, **{f"{n}{f}": 1.1 for n in ("fh", "fhc") for f in range(FPI)},
        **{f"fg{b}": 1.05 for b in range(NB)}, **{f"fs{b}{k}": 1.5 for b in range(NB) for k in (0, 4)}}
WEIGHT = {"pe": 1.0, "dve": 1.0, "act": 0.8, "pool": 0.8, "sp": 0.3}

MX, TDM, UU, LAM = [CC * n for n in range(4)]
NVEC = LAM + CC * NS
IDN, TRI, ONE = 0, P, 2 * P
NCONST = 3 * P
RANK8 = 0
TILE_AT = RANK8 + E * NT
TILE_NO = TILE_AT + E * NT
NROUTE = TILE_NO + FT * (E - 1)
CODES = NS * TOK


class Flow:

    def __init__(self, nc, make_sem, known):
        self.nc, self.make_sem, self.known = nc, make_sem, known
        self.sems, self.count, self.table, self.per_turn, self.turns = {}, {}, {}, {}, {}
        self.stream, self.place, self.i, self.seen = "setup", "once", None, {}
        self.asked, self.clock, self.at, self.cost = None, {}, {}, 0.0
        if known:
            for key, lead in known["lead"].items():
                if lead:
                    nc.sync.sem_inc(self.sem(key), lead * self.unit(key))

    def unit(self, key):
        return 16 if key.startswith("q_") else 1

    def sem(self, key):
        if key not in self.sems:
            self.sems[key] = self.make_sem("s_" + key)
            self.count[key] = 0
        return self.sems[key]

    def done(self, e, name, ins):
        key = e if e.startswith("q_") else f"{self.stream}_{e}"
        ins.then_inc(self.sem(key), self.unit(key))
        self.count[key] += 1
        self.table[self.place, name] = (key, self.count[key])
        e = "pool" if e.startswith("q_fg") else e
        begin = max(self.clock.get(e, 0.0), self.clock.get("sp", 0.0) if e.startswith("q_") else 0.0)
        self.clock[e] = begin + (self.cost if e == "pe" else COST.get(name.split(".")[0], 0.5))
        self.at[name] = self.clock[e]
        if e == "pe":
            self.cost = 0.0
        return ins

    def wait(self, eng, *names):
        ename = {"PE": "pe", "DVE": "dve", "Activation": "act", "Pool": "pool"}.get(str(eng.engine).split(".")[-1], "sp")
        for name in names:
            if not isinstance(name, tuple) or not name[1]:
                name = name if isinstance(name, str) else name[0]
                if self.asked is not None:
                    self.asked.append((name, ename))
                if name in self.at:
                    self.clock[ename] = max(self.clock.get(ename, 0.0), self.at[name] + 0.2)
        if not self.known:
            return
        need = {}
        for name in names:
            name, lag = name if isinstance(name, tuple) else (name, 0)
            assert lag or self.asked is None or (self.place, name) not in self.known["table"] or (self.place, name) in self.table, name
            if lag and self.place == "pre":
                continue
            place = {"last": "main"}.get(self.place, self.place) if lag else self.place
            if "/" in name:
                place, name = name.split("/")
            if (place, name) not in self.known["table"]:
                place = "once" if ("once", name) in self.known["table"] else "pre"
            key, c = self.known["table"][place, name]
            c += self.known["lead"].get(key, 0)
            k = self.known["per_turn"].get(place, {}).get(key, 0)
            if place == self.place:
                c -= lag * k
            elif k:
                c += (self.known["turns"][place] - max(lag, 1)) * k
            turning = bool(k) and place == self.place
            assert c > 0
            need[key, turning] = max(need.get((key, turning), 0), c)
        for (key, turning), c in need.items():
            mark = (eng.engine, key, turning)
            if self.seen.get(mark, -1) >= c:
                continue
            self.seen[mark] = c
            u = self.unit(key)
            if turning:
                eng.wait_ge(self.sem(key), self.i * (self.known["per_turn"][self.place][key] * u) + c * u)
            else:
                eng.wait_ge(self.sem(key), c * u)

    def enter(self, place, turns=1, i=None):
        self.place, self.i, self.seen = place, i, {}
        self.turns[place] = turns
        self.before = dict(self.count)

    def leave(self):
        if self.i is not None:
            k = {e: self.count[e] - self.before.get(e, 0) for e in self.count}
            self.per_turn[self.place] = {e: n for e, n in k.items() if n}
            for e, n in k.items():
                self.count[e] += n * (self.turns[self.place] - 1)
        self.place, self.i, self.seen = "once", None, {}

    def summary(self):
        lead = {}
        for k in self.per_turn.values():
            for e, n in k.items():
                lead[e] = max(lead.get(e, 0), n)
        return {"table": self.table, "per_turn": self.per_turn, "turns": self.turns, "lead": lead, "steps": self.steps}


def program(nc, io, known):
    pe, dve, act, pool, sp = nc.tensor, nc.vector, nc.scalar, nc.gpsimd, nc.sync
    with ExitStack() as ctx:
        def sb(name, shape, dt=F32):
            return ctx.enter_context(nc.sbuf_tensor(name, shape, dt))

        def sem(name):
            return ctx.enter_context(nc.semaphore(name))

        xnT = sb("xnT", [P, CC, NB, T + 1])
        w1 = sb("w1", [P, E * CC * HID])
        w2 = sb("w2", [P, E * HC * C])
        b1c = sb("b1c", [P, E * HC])
        bst = sb("bst", [P, NS, C], F32R)
        tdA = sb("tdA", [P, CC, TDR])
        tdB = sb("tdB", [TDR, C])
        wk, wr, wv, wo = (sb(n, [P, CC, C]) for n in ("wk", "wr", "wv", "wo"))
        wg1 = sb("wg1", [P, CC, GR])
        wg2 = sb("wg2", [P, 2, C])
        vec = sb("vec", [P, NVEC])
        gab = sb("gab", [P, 2, C])
        con = sb("con", [P, NCONST])
        msk = sb("msk", [P, len(LEVELS), LEAF], U32)
        brc = sb("brc", [E, 1])
        S = sb("S", [P, 2, UB * CC, P])
        slot = sb("slot", [P, NT], I32)
        prob = sb("prob", [P, NT])
        expert = sb("expert", [1, FT], I32)
        small = sb("small", [P, 96])

        craw = sb("craw", [P, NS, UN])
        cd = sb("cd", [P, 2, NS, UN], F32R)
        mix = sb("mix", [P, 3, CC, UB, P])
        ba = sb("ba", [P, CC, UB, P])
        R = sb("R", [P, 2, CC, UB, P])
        K = sb("K", [P, 2, CC, UB, P])
        D = sb("D", [P, 2, 2 * CC * UN])
        V = sb("V", [P, 2, UB, C])
        tg = sb("tg", [P, 2, 2, UN])
        tw = sb("tw", [TDR, UN])
        AT = sb("AT", [P, 2, H2, CC, UB, P])
        AP_ = sb("AP_", [P, H2, CC, UB, LEAF])
        Ku = sb("Ku", [P, CC, UB, P])
        sq = sb("sq", [P, UB, C])
        yn = sb("yn", [P, UB, C])
        z = sb("z", [P, UB, C])
        Kt, zT = yn, sq
        res = sb("res", [P, 2, UB, C])
        xs = sb("xs", [P, 2, C])
        xsT = sb("xsT", [P, CC, P])
        hs = sb("hs", [P, HID])
        hsT = sb("hsT", [P, HC, P])
        ys = sb("ys", [P, C])
        b2t = sb("b2t", [P, 2, C])
        gn2 = sb("gn2", [P, 2, UB * GROUPS])
        gv, gy = (gn2[:, n, :] for n in range(2))

        PS = [ctx.enter_context(nc.psum_tensor(f"PS{n}", [P, 512], F32)) for n in range(8)]
        G = PS[0:2]
        FA, FB = PS[2], PS[3]
        L = PS[4:6]
        Y, BB = PS[6], PS[7]

        xs_d = nc.dram_tensor("xs_d", [NB * ZT * P, C], F32, kind="Internal").ap()
        ys_d = nc.dram_tensor("ys_d", [FT * P, C], F32, kind="Internal").ap()
        cd_d = nc.dram_tensor("cd_d", [LORA, CODES + P * NCH], F32, kind="Internal").ap()
        at_d = nc.dram_tensor("at_d", [TOK, C], F32, kind="Internal").ap()

        fl = Flow(nc, sem, known)
        done, wait = fl.done, fl.wait
        fl.steps = {}
        carrier = sem("carrier")

        def settle(eng):
            eng.sem_inc(carrier, 1)

        def interleave(tag, *streams):
            steps = {n: [] for n, _ in streams}
            old = known["steps"][fl.place, tag] if known else {n: [] for n, _ in streams}
            total = {n: sum(step[0] for step in old[n]) + 0.01 for n in old}
            spent = {n: 0.0 for n in old}
            live = dict(streams)
            fl.clock, fl.at = {}, {}
            while live:
                now = fl.clock.get("pe", 0.0)
                best = None
                for n in live:
                    k = len(steps[n])
                    stall = 0.0
                    if known and k < len(old[n]):
                        asked = old[n][k][1]
                        if any((fl.place, a) in known["table"] and (fl.place, a) not in fl.table and a not in old[n][k][2] for a, _ in asked):
                            continue
                        for a, e in asked:
                            if a in fl.at and a not in old[n][k][2]:
                                stall = max(stall, WEIGHT[e] * (fl.at[a] + 0.2 - max(now, fl.clock.get(e, 0.0))))
                    score = (max(stall - 0.3, 0.0), spent[n] / total[n])
                    if best is None or score < best[0]:
                        best = (score, n)
                n = best[1]
                fl.stream, fl.asked = n, []
                k = len(steps[n])
                fl.cost = old[n][k][0] if k < len(old[n]) else 0.0
                before = set(fl.table)
                try:
                    cost = next(live[n])
                except StopIteration:
                    cost = 0.0
                    del live[n]
                spent[n] += cost
                own = {a for p_, a in set(fl.table) - before}
                steps[n].append((cost, fl.asked, own))
            fl.asked = None
            fl.steps[fl.place, tag] = steps

        def cvec(col, cc):
            return vec[:, col + cc:col + cc + 1]

        ident = con[:, IDN:IDN + P]

        aT = AT[:, 0].rearrange("p h c b n -> p (h c b n)")
        aT1 = AT[:, 1].rearrange("p h c b n -> p (h c b n)")
        rout = aT1[:, 0:NROUTE]
        xin = [R[:, :, :, :, :].rearrange("p u c b n -> p (u c b n)").rearrange("p (t c) -> p t c", c=C),
               K[:, :, :, :, :].rearrange("p u c b n -> p (u c b n)").rearrange("p (t c) -> p t c", c=C)]
        xno = [aT.rearrange("p (t c) -> p t c", c=C),
               V[:, :, :, :].rearrange("p u b n -> p (u b n)").rearrange("p (t c) -> p t c", c=C)]
        xxb = [D[:, u, :].rearrange("p (c n) -> p c n", c=CC) for u in range(2)]
        xtok = w2[:, 0:NT * C].rearrange("p (n c) -> p n c", n=NT)
        lgT = [sq[0:E, :, :].rearrange("p b n -> p (b n)"), z[0:E, :, :].rearrange("p b n -> p (b n)")]
        lgs = hs[:, 0:NT * E]
        wA = tg[:, 0, :, :].rearrange("p r n -> p (r n)")[:, 0:CC * GR].rearrange("p (c n) -> p c n", c=CC)
        wrt = hs[:, 256:256 + CC * E].rearrange("p (c n) -> p c n", c=CC)
        hcode = [w1[LORA * k:LORA * (k + 1), 0:NS * 512] for k in range(2)]
        braw = mix[:, :, :, :, :].rearrange("p s c b n -> p (s c b n)")[:, 0:NS * C].rearrange("p (s n) -> p s n", s=NS)
        xdr = io["x"].rearrange("(b h t p) c -> b h p t c", b=NB, h=2, t=4)

        for dst, src in ((con[:, :], io["con"]), (vec[:, :], io["vec"]), (brc[:, :], io["br"]),
                         (wrt, io["Wr"].rearrange("(c p) n -> p c n", p=P))):
            done("q_c1", "c1", act.dma_start(dst, src))
        done("q_c1", "c1", act.dma_start(wA, io["A"].rearrange("(c p) n -> p c n", p=P)))
        for q in range(4):
            done("q_c2", "c2", act.dma_start(braw[LORA * q:LORA * (q + 1), :, :], io["Bp"].rearrange("s r c -> r s c")))
        done("q_c2", "c2", act.dma_start(rout, io["rout"]))

        for dst, src in (
                (tdA[:, :, :], io["tdA"].rearrange("(c p) n -> p c n", p=P)), (tdB[:, :], io["tdB"]),
                (wk[:, :, :], io["WkT"].rearrange("(c p) n -> p c n", p=P)),
                (wv[:, :, :], io["WvT"].rearrange("(c p) n -> p c n", p=P)),
                (wr[:, :, :], io["WrT"].rearrange("(c p) n -> p c n", p=P)),
                (wg1[:, :, :], io["Wg1"].rearrange("(c p) n -> p c n", p=P)),
                (wo[:, :, :], io["WoT"].rearrange("(c p) n -> p c n", p=P)),
                (wg2[:, 0, :], io["Wg2"][0:P, :]), (wg2[0:GR - P, 1, :], io["Wg2"][P:GR, :]),
                (gab[:, 0, :], io["gamma"].partition_broadcast(P)), (gab[:, 1, :], io["beta"].partition_broadcast(P)),
                (msk[:, :, :], io["msk"])):
            done("q_w", "w", act.dma_start(dst, src))

        mhalf = small[:, 59:60]
        done("pool", "mhalf", pool.memset(mhalf, -0.5))
        done("pool", "z_x0", pool.memset(xnT[:, :, :, 0:1], 0.0))
        done("pool", "z_hsT", pool.memset(hsT[:, :, :], 0.0))
        wait(pool, "mhalf")

        wait(dve, "z_x0")
        zsrc = hsT[:, :, :].rearrange("p (o h) n -> p o (h n)", o=1)
        wait(sp, "z_hsT")

        def zeros(b):
            done("q_zero", "zero", sp.dma_start(xs_d[bass.ds(b * (ZT * P), ZT * P), :].rearrange("(p a r) c -> p a (r c)", a=ZT // 2, r=2),
                                                zsrc.broadcast_to([P, ZT // 2, 2 * C])))
            yield 0.0

        def first(b, hf):
            wait(sp, (f"xn{hf}", 1))
            done(f"q_x{hf}", f"x{hf}", sp.dma_start(xin[hf], xdr[bass.ds(b, 1), hf, :, :, :]))
            yield 0.0
            st = small[:, 64 * hf:64 * hf + 24].rearrange("p (t s) -> p t s", t=4)
            mv = small[:, 24 + 12 * hf:32 + 12 * hf].rearrange("p (t s) -> p t s", t=4)
            rs = small[:, 32 + 12 * hf:36 + 12 * hf]
            wait(dve, f"x{hf}")
            for t in range(4):
                i1 = dve.bn_stats(st[:, t, :], xin[hf][:, t, :])
            done("dve", f"bn{hf}", i1)
            wait(dve, f"bn{hf}")
            settle(dve)
            for t in range(4):
                i1 = dve.bn_aggr(mv[:, t, :], st[:, t, :])
            done("dve", f"ag{hf}", i1)
            wait(dve, f"ag{hf}")
            done("dve", f"ve{hf}", dve.tensor_scalar(rs, mv[:, :, 1], EPS_LN, None, ALU.add))
            wait(pool, f"ve{hf}")
            done("pool", f"rs{hf}", pool.tensor_tensor(rs, rs, mhalf[:, 0:1].broadcast_to([P, 4]), ALU.pow))
            yield 0.0
            wait(dve, f"rs{hf}", (f"tr{hf}", 1), (f"xt{hf}", 1))
            for t in range(4):
                i1 = dve.tensor_scalar(xno[hf][:, t, :], xin[hf][:, t, :], mv[:, t, 0:1], rs[:, t:t + 1], ALU.subtract, ALU.mult)
            done("dve", f"xn{hf}", i1)
            wait(pool, f"xn{hf}")
            done("pool", f"xt{hf}", pool.tensor_copy(xtok[:, bass.ds(b * 8 + 4 * hf, 4), :], xno[hf]))
            yield 0.0
            bank = [G[0], G[1]] if hf == 0 else [FA, FB]
            wait(pe, f"xn{hf}", (f"h{hf}", 1), "c1")
            for cc in range(CC):
                for t in range(4):
                    i1 = pe.transpose(bank[cc][:, P * t:P * (t + 1)], xno[hf][:, t, cc * P:(cc + 1) * P], ident)
            done("pe", f"tr{hf}", i1)
            wait(act, f"tr{hf}")
            span = slice(1 + 512 * hf, 1 + 512 * (hf + 1))
            for cc in range(CC):
                i1 = act.activation(xnT[:, cc, bass.ds(b, 1), span].rearrange("p o n -> p (o n)"), bank[cc][:, :], ACT.Copy)
            done("act", f"tc{hf}", i1)
            yield 0.9
            wait(pe, f"tc{hf}", (f"lc{hf}", 1))
            for cc in range(CC):
                i1 = pe.matmul(L[hf][0:E, :], wrt[:, cc, :], xnT[:, cc, bass.ds(b, 1), span].rearrange("p o n -> p (o n)"),
                               start=(cc == 0), stop=(cc == CC - 1))
            done("pe", f"lg{hf}", i1)
            wait(act, f"lg{hf}", (f"lt{hf}", 1), "c1")
            done("act", f"lc{hf}", act.activation(lgT[hf], L[hf][0:E, :], ACT.Identity, bias=brc[:, 0:1]))
            yield 1.7
            span0 = slice(512 * hf, 512 * (hf + 1))
            xx = xxb[hf]
            xrow = xnT[:, :, bass.ds(b, 1), span].rearrange("p c o n -> p (c o) n")
            wait(dve, f"tc{hf}", (f"hm{hf}", 1))
            done("dve", f"xd{hf}", dve.tensor_tensor(xx, xnT[:, :, bass.ds(b, 1), span0].rearrange("p c o n -> p (c o) n"), xrow, ALU.subtract))
            wait(dve, f"xd{hf}")
            for cc in range(CC):
                i1 = dve.scalar_tensor_tensor(xx[:, cc, :], xx[:, cc, :], cvec(MX, cc), xnT[:, cc, bass.ds(b, 1), span].rearrange("p o n -> p (o n)"), ALU.mult, ALU.add)
            done("dve", f"xx{hf}", i1)
            yield 0.0
            cb = [G[0], G[1]] if hf == 0 else [FA, FB]
            wait(pe, f"xx{hf}", f"tc{hf}")
            for cc in range(CC):
                pe.matmul(cb[0][:, :], wA[:, cc, 0:P], xx[:, cc, :], start=(cc == 0), stop=(cc == 1))
            for cc in range(CC):
                i1 = pe.matmul(cb[1][0:LORA, :], wA[:, cc, P:GR], xx[:, cc, :], start=(cc == 0), stop=(cc == 1))
            done("pe", f"hm{hf}", i1)
            wait(act, f"hm{hf}", (f"cs{hf}", 1))
            for g in range(NS):
                src = cb[0][LORA * g:LORA * (g + 1), :] if g < 4 else cb[1][0:LORA, :]
                i1 = act.activation(hcode[hf][:, g:NS * 511 + g + 1:NS], src, ACT.Tanh)
            done("act", f"h{hf}", i1)
            wait(act, f"h{hf}")
            done(f"q_cs{hf}", f"cs{hf}", act.dma_start(cd_d[:, bass.ds(b * (NS * T) + hf * (NS * 512), NS * 512)], hcode[hf]))
            yield 3.4
            lb = Y if hf == 0 else BB
            wait(pe, f"lc{hf}", (f"ls{hf}", 1))
            settle(pe)
            for t in range(4):
                i1 = pe.transpose(lb[:, E * t:E * (t + 1)], lgT[hf][:, P * t:P * (t + 1)], con[0:E, IDN:IDN + E])
            done("pe", f"lt{hf}", i1)
            wait(act, f"lt{hf}")
            done("act", f"ls{hf}", act.activation(lgs[:, bass.ds((b * 8 + 4 * hf) * E, 4 * E)], lb[:, 0:4 * E], ACT.Copy))

        with nc.Fori(0, NB) as b:
            fl.enter("ln", NB, b)
            interleave("a", ("ln0", first(b, 0)), ("ln1", first(b, 1)), ("zero", zeros(b)))
            fl.leave()
        fl.stream = "setup"

        pool.memset(S[:, :, :, :], 0.0)
        done("pool", "z_S", pool.memset(AP_[:, :, :, :, :], 0.0))
        done("q_zero2", "zero2", sp.dma_start(cd_d[:, CODES:CODES + P], zsrc[0:LORA, 0, 0:P]))
        wait(dve, "c2")
        done("dve", "bhi", dve.tensor_copy(bst[:, :, :], braw))
        wait(dve, "bhi")
        for q in (1, 3):
            i1 = dve.tensor_tensor(bst[LORA * q:LORA * (q + 1), :, :], braw[LORA * q:LORA * (q + 1), :, :],
                                   bst[LORA * q:LORA * (q + 1), :, :].bitcast(F32), ALU.subtract)
        done("dve", "bst", i1)
        mwv = small[:, 48:56]
        wv3 = wv[:, :, :].rearrange("p c (h i) -> p (c h) i", i=HEAD)
        wait(dve, "w")
        done("dve", "wv_s", dve.tensor_reduce(mwv, wv3, AX.X, ALU.add))
        wait(dve, "wv_s")
        done("dve", "wv_m", dve.tensor_scalar(mwv, mwv, 1.0 / HEAD, None, ALU.mult))
        wait(dve, "wv_m")
        done("dve", "wv_c", dve.tensor_tensor(wv3, wv3, mwv.rearrange("p (g o) -> p g o", o=1).broadcast_to([P, CC * GROUPS, HEAD]), ALU.subtract))

        def routing():
            def area(n):
                return res[:, n // 2, :, :].rearrange("p b c -> p (b c)")[:, 256 * (n % 2):256 * (n % 2) + 256].rearrange("p (t e) -> p t e", e=E)

            ex, oh, pre, tot = (area(n) for n in range(4))
            Lg = lgs.rearrange("p (t e) -> p t e", e=E)
            m1 = small[:, 0:NT]

            def bc(a):
                return a.rearrange("p (t o) -> p t o", o=1).broadcast_to([P, NT, E])

            def step(name, ins):
                done("dve", name, ins)
                wait(dve, name)

            wait(dve, "ln/ls1", "ln/xn1")
            step("r_max", dve.tensor_reduce(m1, Lg, AX.X, ALU.max))
            step("r_sub", dve.tensor_tensor(ex, Lg, bc(m1), ALU.subtract))
            wait(act, "r_sub")
            done("act", "r_exp", act.activation(ex, ex, ACT.Exp))
            yield 0.0
            wait(dve, "r_exp")
            step("r_sum", dve.tensor_reduce(m1, ex, AX.X, ALU.add))
            step("r_rec", dve.reciprocal(m1, m1))
            step("r_prb", dve.tensor_tensor(ex, ex, bc(m1), ALU.mult))
            yield 0.0
            step("r_pmx", dve.tensor_reduce(prob[:, :], ex, AX.X, ALU.max))
            step("r_eq", dve.tensor_tensor(oh, ex, bc(prob[:, :]), ALU.is_equal))
            wait(dve, "c2")
            rank8 = rout[:, RANK8:RANK8 + NT * E].rearrange("p (t e) -> p t e", e=E)
            step("r_rk", dve.tensor_tensor(oh, oh, rank8, ALU.mult))
            yield 0.0
            step("r_rm", dve.tensor_reduce(m1, oh, AX.X, ALU.max))
            step("r_oh", dve.tensor_tensor(oh, rank8, bc(m1), ALU.is_equal))
            wait(pe, "r_oh", "c2")
            ohf = oh.rearrange("p t e -> p (t e)")
            pe.matmul(FA[:, 0:NT * E], con[:, TRI:TRI + P], ohf, start=True, stop=True)
            done("pe", "r_mm", pe.matmul(FB[:, 0:NT * E], con[:, ONE:ONE + P], ohf, start=True, stop=True))
            yield 0.0
            wait(dve, "r_mm")
            dve.tensor_copy(pre, FA[:, 0:NT * E].rearrange("p (t e) -> p t e", e=E))
            step("r_tot", dve.tensor_copy(tot, FB[:, 0:NT * E].rearrange("p (t e) -> p t e", e=E)))
            for e in range(E):
                i1 = dve.tensor_tensor_scan(ex[:, :, e], tot[:, :, e], tot[:, :, e], 0.0, ALU.add, ALU.bypass)
            step("r_scan", i1)
            yield 0.0
            cnt = ex[:, NT - 1, :]
            tl = small[:, 32:40]
            en = small[:, 40:48]
            cmp = lgs.rearrange("p (e j) -> p e j", e=E)
            tile_at = rout[:, TILE_AT:TILE_AT + E * NT].rearrange("p (e j) -> p e j", e=E)
            step("r_cmp", dve.tensor_tensor(cmp, cnt.rearrange("p (e o) -> p e o", o=1).broadcast_to([P, E, NT]), tile_at, ALU.is_gt))
            step("r_tl", dve.tensor_reduce(tl, cmp, AX.X, ALU.add))
            step("r_en", dve.tensor_tensor_scan(en, tl, tl, 0.0, ALU.add, ALU.bypass))
            step("r_s0", dve.tensor_tensor(tl, en, tl, ALU.subtract))
            step("r_s1", dve.tensor_scalar(tl, tl, float(P), None, ALU.mult))
            yield 0.0
            step("r_s2", dve.tensor_tensor(pre, pre, ex, ALU.add))
            step("r_s3", dve.tensor_tensor(pre, pre, tot, ALU.subtract))
            step("r_s4", dve.tensor_tensor(pre, pre, tl.rearrange("p (o e) -> p o e", o=1).broadcast_to([P, NT, E]), ALU.add))
            yield 0.0
            step("r_s5", dve.tensor_tensor(pre, pre, oh, ALU.mult))
            step("r_s6", dve.tensor_reduce(m1, pre, AX.X, ALU.add))
            done("dve", "r_slot", dve.tensor_copy(slot[:, :], m1))
            wait(pool, "r_slot", "ln/zero", "ln/xt0", "ln/xt1")
            for t in range(NT):
                done("q_scat", "scat", pool.indirect_dma_start(xs_d, bass.IndirectOffsetOnAxis(slot[:, t:t + 1], 0), xtok[:, t, :], None))
            yield 0.0
            tno = rout[0:1, TILE_NO:TILE_NO + FT * (E - 1)].rearrange("p (j e) -> p j e", e=E - 1)
            w2c = res[0:1, 1, :, :].rearrange("p b c -> p (b c)")[:, 0:FT * (E - 1)].rearrange("p (j e) -> p j e", e=E - 1)
            ef = small[0:1, 0:FT]
            step("r_c2", dve.tensor_tensor(w2c, tno, en[0:1, 0:E - 1].rearrange("p (o e) -> p o e", o=1).broadcast_to([1, FT, E - 1]), ALU.is_ge))
            step("r_ef", dve.tensor_reduce(ef, w2c, AX.X, ALU.add))
            step("r_ex", dve.tensor_copy(expert[:, :], ef))
            yield 0.0

        fl.stream = "front"
        xres = io["x"].rearrange("(u b k p) c -> k u p b c", u=2, b=UB, k=NCH)
        aout = at_d.rearrange("(u b k p) c -> k u p b c", u=2, b=UB, k=NCH)

        def codes(u, c):
            first = fl.place == "once"
            if not first:
                wait(sp, "clo.1" if u == 0 else "once/clo.0" if fl.place == "pre" else ("clo.0", 1))
            src = cd_d[:, bass.ds(c * P, CODES)].rearrange("r (s b t) -> r s b t", s=NS, b=NB)
            for q in range(4):
                for b in range(UB):
                    done("q_cr", f"cr.{u}", sp.dma_start(craw[LORA * q:LORA * (q + 1), :, b * P:(b + 1) * P], src[:, :, UB * u + b, 0:P]))
            yield 0.0
            wait(act, f"cr.{u}", *([] if first else [(f"mm4.{u}", 1 if u else 0)]))
            done("act", f"chi.{u}", act.activation(cd[:, u, :, :], craw[:, :, :], ACT.Copy))
            yield 0.0
            wait(dve, f"chi.{u}")
            done("dve", f"clo.{u}", dve.tensor_tensor(cd[P // 2:P, u, :, :], craw[P // 2:P, :, :], cd[P // 2:P, u, :, :].bitcast(F32), ALU.subtract))
            yield 0.0

        CHUNK_TOT = sum(CC * UN // B for B in (1, 2, 4, 8, 16, 32, 64))

        def fl2(a):
            return a.rearrange("p c b n -> p (c b n)")

        FRONT_USES = ("m0", "m1", "tw", "m2", "d", "k", "m3", "v", "m4", "r", "tg")

        def front(u, c):
            o = 1 - u
            pre = fl.place == "pre"
            other = lambda name: (f"{name}.{o}", 1 if u == 0 else 0)
            pairs_ = lambda name: (f"{name}.{u}", 1 if u == 0 or pre else 0)
            tail_ = lambda name: (f"{name}.{u}", 1 if pre else 0)
            uses = []
            if not (pre and u == 0):
                wait(pe, ("clo.0", 1) if u == 0 else "clo.1")

            def bank(name):
                n = len(uses)
                assert FRONT_USES[n] == name
                uses.append(name)
                wait(pe, f"{FRONT_USES[n - 2]}.{u}" if n > 1 else other(FRONT_USES[n - 2]))
                return G[(n + u) % 2]

            xc = xnT[:, :, UB * u:UB * (u + 1), bass.ds(c * P + 1, P)]
            xp = xnT[:, :, UB * u:UB * (u + 1), bass.ds(c * P, P)]
            adds, adder = ("dve", dve) if pre else ("pool", pool)
            wait(adder, other("m4"))
            settle(adder)
            done(adds, f"ba.{u}", adder.tensor_tensor(ba[:, :, :, :], xp, xc, ALU.subtract))
            readers = {0: other("rm"), 1: other("gm"), 2: other("vm"), 3: f"tA.{u}", 4: f"km.{u}"}

            def mixed(s):
                bk = bank(f"m{s}")
                for cc in range(CC):
                    i1 = pe.matmul(bk[:, cc * UN:(cc + 1) * UN], bst[:, s, cc * P:(cc + 1) * P], cd[:, u, s, :], start=True, stop=True)
                done("pe", f"mm{s}.{u}", i1)
                buf = mix[:, s % 3, :, :, :]
                wait(dve, f"mm{s}.{u}", f"ba.{u}", readers[s])
                for cc in range(CC):
                    i1 = dve.scalar_tensor_tensor(
                        buf[:, cc, :, :].rearrange("p b n -> p (b n)"), bk[:, cc * UN:(cc + 1) * UN],
                        vec[:, LAM + CC * s + cc:LAM + CC * s + cc + 1], ba[:, cc, :, :].rearrange("p b n -> p (b n)"), ALU.add, ALU.mult)
                done("dve", f"m{s}.{u}", i1)
                wait(adder, f"m{s}.{u}")
                settle(adder)
                done(adds, f"x{s}.{u}", adder.tensor_tensor(buf, buf, xc, ALU.add))

            def src(s, cc):
                return mix[:, s % 3, cc, :, :].rearrange("p b n -> p (b n)")

            mixed(0)
            yield 0.25
            mixed(1)
            yield 0.25
            bk = bank("tw")
            wait(pe, f"x0.{u}")
            for cc in range(CC):
                i1 = pe.matmul(bk[0:TDR, 0:UN], tdA[:, cc, :], src(0, cc), start=(cc == 0), stop=(cc == 1))
            done("pe", f"tA.{u}", i1)
            wait(act, f"tA.{u}", other("tB"))
            done("act", f"tw.{u}", act.activation(tw[:, :], bk[0:TDR, 0:UN], ACT.Tanh))
            yield 0.25
            mixed(2)
            yield 0.25
            bk = bank("d")
            wait(pe, f"tw.{u}")
            for cc in range(CC):
                i1 = pe.matmul(bk[:, cc * UN:(cc + 1) * UN], tdB[:, cc * P:(cc + 1) * P], tw[:, :], start=True, stop=True)
            done("pe", f"tB.{u}", i1)
            wait(act, f"tB.{u}", pairs_("gr1"))
            for cc in range(CC):
                i1 = act.activation(D[:, u, cc * UN:(cc + 1) * UN], bk[:, cc * UN:(cc + 1) * UN], ACT.Exp, bias=cvec(TDM, cc))
            done("act", f"d.{u}", i1)
            yield 0.9

            def project(w, s, bk):
                for co in range(CC):
                    for cc in range(CC):
                        i1 = pe.matmul(bk[:, co * UN:(co + 1) * UN], w[:, cc, co * P:(co + 1) * P], src(s, cc), start=(cc == 0), stop=(cc == 1))
                return i1

            bk = bank("k")
            wait(pe, f"x1.{u}")
            done("pe", f"km.{u}", project(wk, 1, bk))
            wait(dve, f"km.{u}", f"d.{u}", tail_("kT"))
            done("dve", f"k.{u}", dve.scalar_tensor_tensor(fl2(K[:, u]), D[:, u, 0:CC * UN], 1.0, bk[:, :], ALU.min, ALU.mult))
            yield 1.7
            mixed(3)
            yield 0.25
            bk = bank("v")
            wait(pe, f"x2.{u}")
            for b in range(UB):
                for cc in range(CC):
                    i1 = pe.matmul(bk[:, b * C:(b + 1) * C], mix[:, 2, cc, b, :], wv[:, cc, :], start=(cc == 0), stop=(cc == 1))
            done("pe", f"vm.{u}", i1)
            wait(act, f"vm.{u}", tail_("sm"))
            done("act", f"v.{u}", act.activation(V[:, u, :, :].rearrange("p b n -> p (b n)"), bk[:, :], ACT.Copy))
            yield 1.7
            mixed(4)
            yield 0.25
            bk = bank("r")
            wait(pe, f"x3.{u}")
            done("pe", f"rm.{u}", project(wr, 3, bk))
            wait(act, f"rm.{u}", tail_("y"))
            done("act", f"r.{u}", act.activation(fl2(R[:, u]), bk[:, :], ACT.Copy))
            yield 1.7
            bk = bank("tg")
            wait(pe, f"x4.{u}")
            for k, (m0, m1_) in enumerate(((0, P), (P, GR))):
                for cc in range(CC):
                    i1 = pe.matmul(bk[0:m1_ - m0, k * UN:(k + 1) * UN], wg1[:, cc, m0:m1_], src(4, cc), start=(cc == 0), stop=(cc == 1))
            done("pe", f"gm.{u}", i1)
            wait(act, f"gm.{u}", tail_("gg"))
            for k, rows in enumerate((P, GR - P)):
                i1 = act.activation(tg[0:rows, u, k, :], bk[0:rows, k * UN:(k + 1) * UN], ACT.Tanh)
            done("act", f"tg.{u}", i1)
            yield 1.7

        def pairs(u, c):
            lag = 1 if u == 1 else 0
            o = 1 - u
            pre = fl.place == "pre"
            F = lambda name: (f"{name}.{u}", lag)
            before = lambda name: (f"{name}.{o}", 1 if u == 1 or pre else 0)
            tail_ = lambda name: (f"{name}.{u}", 1 if u == 1 or pre else 0)
            Ku_, Ru, Du = K[:, u], R[:, u], D[:, u, :]
            cols = CC * UN

            wait(act, F("k"), before("l01"))
            for cc in range(CC):
                i1 = act.activation(Ku[:, cc, :, :].rearrange("p b n -> p (b n)"), K[:, u, cc, :, :].rearrange("p b n -> p (b n)"),
                                    ACT.Copy, scale=cvec(UU, cc))
            done("act", f"ku.{u}", i1)
            yield 0.0

            def tots(B):
                at = 0 if B == 1 else sum(cols // b for b in (1, 2, 4, 8, 16, 32, 64) if b < B)
                return Du[:, at:at + cols // B]

            def grow(B):
                n = cols // (2 * B)
                half = lambda a: fl2(a).rearrange("p (n h t) -> p n h t", h=2, t=B)
                tt = tots(B).rearrange("p (n h) -> p n h", h=2)
                wide = lambda a: a.rearrange("p (n o) -> p n o", o=1).broadcast_to([P, n, B])
                r2, k2 = half(Ru)[:, :, 1, :], half(Ku_)[:, :, 0, :]
                dve.tensor_tensor(r2, r2, wide(tt[:, :, 0]), ALU.mult)
                dve.tensor_tensor(k2, k2, wide(tt[:, :, 1]), ALU.mult)
                done("dve", f"gr{B}.{u}", dve.tensor_tensor(tots(2 * B), tt[:, :, 0], tt[:, :, 1], ALU.mult))

            for li, B in enumerate(LEVELS):
                if li == 0:
                    wait(pe, f"ku.{u}", F("r"))
                elif B > 1:
                    wait(pe, f"gr{B // 2}.{u}")
                Ks = Ku if li == 0 else Ku_
                for h in range(H2):
                    wait(pe, *([before(f"e64{h}")] if li == 0 else [f"a{li - 1}{h}.{u}"]))
                    settle(pe)
                    rows = slice(HEAD * h, HEAD * (h + 1))
                    for cc in range(CC):
                        for b in range(UB):
                            for q in range(P // LEAF):
                                i1 = pe.matmul(L[h][LEAF * q:LEAF * (q + 1), (cc * UB + b) * LEAF:(cc * UB + b + 1) * LEAF],
                                               Ks[rows, cc, b, LEAF * q:LEAF * (q + 1)], Ru[rows, cc, b, LEAF * q:LEAF * (q + 1)],
                                               start=True, stop=True, tile_position=(HEAD * h, LEAF * q))
                    done("pe", f"l{li}{h}.{u}", i1)
                    wait(dve, f"l{li}{h}.{u}", *([before("spread")] if li == 0 else [f"a{li - 1}{h}.{u}"]))
                    settle(dve)
                    m = msk[:, li:li + 1, :].broadcast_to([P, CC * UB, LEAF])
                    done("dve", f"a{li}{h}.{u}", dve.copy_predicated(
                        AP_[:, h, :, :, :].rearrange("p c b n -> p (c b) n"), m,
                        L[h][:, 0:CC * UB * LEAF].rearrange("p (g n) -> p g n", n=LEAF)))
                    if h == 0:
                        yield 0.7
                if B >= 1:
                    wait(dve, F("d") if B == 1 else f"gr{B // 2}.{u}")
                    grow(B)
                yield 0.7
            for B in (32, 64):
                wait(pe, f"gr{B // 2}.{u}")
                for h in range(H2):
                    wait(pe, f"a{len(LEVELS) - 1}{h}.{u}" if B == 32 else f"e32{h}.{u}")
                    settle(pe)
                    rows = slice(HEAD * h, HEAD * (h + 1))
                    for cc in range(CC):
                        for b in range(UB):
                            for s0 in range(0, P, 2 * B):
                                i1 = pe.matmul(L[h][s0:s0 + B, (cc * UB + b) * B:(cc * UB + b + 1) * B], Ku_[rows, cc, b, s0:s0 + B],
                                               Ru[rows, cc, b, s0 + B:s0 + 2 * B], start=True, stop=True, tile_position=(HEAD * h, s0))
                    done("pe", f"l{B}{h}.{u}", i1)
                    wait(act, f"l{B}{h}.{u}", tail_("y"))
                    for s0 in range(0, P, 2 * B):
                        i1 = act.activation(AT[s0:s0 + B, u, h, :, :, s0 + B:s0 + 2 * B].rearrange("p c b n -> p (c b) n"),
                                            L[h][s0:s0 + B, 0:CC * UB * B].rearrange("p (g n) -> p g n", n=B), ACT.Copy)
                    done("act", f"e{B}{h}.{u}", i1)
                    if h == 0:
                        yield 0.5
                wait(dve, f"gr{B // 2}.{u}", f"l{B}1.{u}", *([tail_("S_dec")] if B == 64 else []))
                grow(B)
                yield 0.5
            wait(act, *[f"a{len(LEVELS) - 1}{h}.{u}" for h in range(H2)])
            for q in range(P // LEAF):
                i1 = act.activation(AT[LEAF * q:LEAF * (q + 1), u, :, :, :, LEAF * q:LEAF * (q + 1)].rearrange("p h c b n -> p (h c b) n"),
                                    AP_[LEAF * q:LEAF * (q + 1), :, :, :, :].rearrange("p h c b n -> p (h c b) n"), ACT.Copy)
            done("act", f"spread.{u}", i1)

            yield 0.0

        def tail(u, c):
            o = 1 - u
            F = lambda name: (f"{name}.{u}", 1)
            pairs_ = lambda name: (f"{name}.{u}", 1 if u == 0 else 0)
            before = lambda name: (f"{name}.{o}", 1 if u == 0 else 0)
            Ru = R[:, u]
            tot = D[:, u, :][:, CHUNK_TOT:CHUNK_TOT + CC * UB]
            flat = lambda a: a[:, :, :].rearrange("p b n -> p (b n)")

            wait(sp, (f"st.{u}", 1))
            done(f"q_res{u}", f"res.{u}", sp.dma_start(res[:, u, :, :], xres[bass.ds(c, 1), u, :, :, :].rearrange("o p b c -> p (o b) c")))

            wait(pe, pairs_("gr64"), before("o"))
            for b in range(UB):
                for cc in range(CC):
                    i1 = pe.transpose(BB[:, b * C + cc * P:b * C + (cc + 1) * P], K[:, u, cc, b, :], ident)
            done("pe", f"kT.{u}", i1)
            yield 0.45
            wait(act, f"kT.{u}", before("z"))
            done("act", f"kt.{u}", act.activation(flat(Kt), BB[:, :], ACT.Copy))

            wait(pe, pairs_("spread"), F("v"), (f"S_new.{u}", 1), before("zc"))
            settle(pe)
            for b in range(UB):
                for cc in range(CC):
                    at = b * C + cc * P
                    pe.matmul(Y[:, at:at + P], Ru[:, cc, b, :], S[:, u, b * CC + cc, :], start=True, stop=False)
                    for h in range(H2):
                        i1 = pe.matmul(Y[:, at + HEAD * h:at + HEAD * (h + 1)], AT[:, u, h, cc, b, :],
                                       V[:, u, b, cc * P + h * HEAD:cc * P + (h + 1) * HEAD], start=False, stop=(h == H2 - 1))
                if b == 0:
                    yield 1.3
            done("pe", f"y.{u}", i1)
            wait(act, f"y.{u}", before("om"))
            done("act", f"sq.{u}", act.activation(flat(sq), Y[:, :], ACT.Square))
            wait(dve, f"y.{u}", pairs_("gr64"))
            for h in range(H2):
                Sh = S[HEAD * h:HEAD * (h + 1), u, :, HEAD * h:HEAD * (h + 1)].rearrange("p (b c) i -> p c b i", b=UB)
                for cc in range(CC):
                    i1 = dve.tensor_tensor(Sh[:, cc], Sh[:, cc], tot[HEAD * h:HEAD * (h + 1), cc * UB:(cc + 1) * UB]
                                           .rearrange("p (b o) -> p b o", o=1).broadcast_to([HEAD, UB, HEAD]), ALU.mult)
            done("dve", f"S_dec.{u}", i1)
            yield 1.3
            wait(pe, f"kt.{u}")
            settle(pe)
            for b in range(UB):
                for cc in range(CC):
                    for h in range(H2):
                        g = b * CC + cc
                        i1 = pe.matmul(BB[HEAD * h:HEAD * (h + 1), g * HEAD:(g + 1) * HEAD],
                                       Kt[:, b, cc * P + HEAD * h:cc * P + HEAD * (h + 1)], V[:, u, b, cc * P + h * HEAD:cc * P + (h + 1) * HEAD],
                                       start=True, stop=True, tile_position=(0, HEAD * h))
            done("pe", f"sm.{u}", i1)
            wait(dve, f"sm.{u}", f"S_dec.{u}")
            for h in range(H2):
                Sh = S[HEAD * h:HEAD * (h + 1), u, :, HEAD * h:HEAD * (h + 1)]
                i1 = dve.tensor_tensor(Sh, Sh, BB[HEAD * h:HEAD * (h + 1), 0:UB * CC * HEAD].rearrange("p (g i) -> p g i", i=HEAD), ALU.add)
            done("dve", f"S_new.{u}", i1)
            yield 0.9

            wait(pe, F("tg"), f"S_new.{u}")
            for b in range(UB):
                o_ = BB[:, b * C:(b + 1) * C]
                pe.matmul(o_, tg[:, u, 0, b * P:(b + 1) * P], wg2[:, 0, :], start=True, stop=False)
                i1 = pe.matmul(o_, tg[0:GR - P, u, 1, b * P:(b + 1) * P], wg2[0:GR - P, 1, :], start=False, stop=True)
            done("pe", f"gg.{u}", i1)
            yield 1.7
            heads = lambda a: a.rearrange("p (g i) -> p g i", i=HEAD)
            wait(dve, f"sq.{u}")
            done("dve", f"va.{u}", dve.tensor_reduce(gv, heads(flat(sq)), AX.X, ALU.add))
            wait(dve, f"va.{u}")
            done("dve", f"gv.{u}", dve.tensor_scalar(gv, gv, 1.0 / HEAD, EPS_GN, ALU.mult, ALU.add))
            wait(pool, f"gv.{u}")
            done("pool", f"gy.{u}", pool.tensor_tensor(gy, gv, mhalf[:, 0:1].broadcast_to([P, UB * GROUPS]), ALU.pow))
            yield 0.0
            wait(dve, f"gy.{u}", f"sm.{u}")
            done("dve", f"yg.{u}", dve.tensor_tensor(heads(flat(yn)), heads(Y[:, :]), gy.rearrange("p (g o) -> p g o", o=1).broadcast_to([P, UB * GROUPS, HEAD]), ALU.mult))
            both = lambda n: gab[:, n:n + 1, :].broadcast_to([P, UB, C])
            does, doer = ("dve", dve) if fl.place == "last" else ("pool", pool)
            wait(doer, f"yg.{u}")
            done(does, f"ym.{u}", doer.tensor_tensor(yn[:, :, :], yn[:, :, :], both(0), ALU.mult))
            wait(doer, f"ym.{u}")
            done(does, f"yb.{u}", doer.tensor_tensor(yn[:, :, :], yn[:, :, :], both(1), ALU.add))
            yield 0.0
            wait(dve, f"gg.{u}", f"yb.{u}")
            done("dve", f"z.{u}", dve.tensor_tensor(flat(z), flat(yn), BB[:, :], ALU.mult))
            yield 0.0
            wait(pe, f"z.{u}")
            for b in range(UB):
                for cc in range(CC):
                    i1 = pe.transpose(Y[:, b * C + cc * P:b * C + (cc + 1) * P], z[:, b, cc * P:(cc + 1) * P], ident)
            done("pe", f"zt.{u}", i1)
            wait(act, f"zt.{u}")
            done("act", f"zc.{u}", act.activation(flat(zT), Y[:, :], ACT.Copy))
            yield 0.45
            wait(pe, f"zc.{u}")
            for b in range(UB):
                for cc in range(CC):
                    i1 = pe.matmul(BB[:, b * C:(b + 1) * C], zT[:, b, cc * P:(cc + 1) * P], wo[:, cc, :], start=(cc == 0), stop=(cc == 1))
            done("pe", f"om.{u}", i1)
            wait(dve, f"om.{u}", f"res.{u}")
            r2 = res[:, u, :, :].rearrange("p b n -> p (b n)")
            done("dve", f"o.{u}", dve.tensor_tensor(r2, r2, BB[:, :], ALU.add))
            if fl.place != "last":
                wait(sp, f"o.{u}")
                done(f"q_st{u}", f"st.{u}", sp.dma_start(aout[bass.ds(c, 1), u, :, :, :].rearrange("o p b c -> p (o b) c"), res[:, u, :, :]))
            yield 1.7

        def experts(first, tiles):
            for f in range(tiles):
                was = (lambda n: (f"{n}{FPI - 1}", 1)) if f == 0 else (lambda n: f"{n}{f - 1}")
                ahead = ([0] if f == 0 else []) + ([f + 1] if f + 1 < tiles else [])
                for g in ahead:
                    k = g % 2
                    user = g - 2 if g > 1 else max(n for n in range(FPI) if n % 2 == k)
                    lag = 0 if g > 1 else 1
                    wait(sp, (f"fxt{user}", lag), (f"fy{user}", lag))
                    if g:
                        done(f"q_xs{k}", f"xs{g}", sp.dma_start(xs[:, k, :], xs_d[bass.ds(first * P + g * P, P), :]))
                    sv = sp.value_load(expert[0:1, bass.ds(first + g, 1)], min_val=0, max_val=E - 1)
                    done(f"q_b2{k}", f"b2{g}", sp.dma_start(b2t[:, k, :], io["b2"][bass.ds(sv * C, C)].partition_broadcast(P)))
                wait(pe, ("xs0", 1) if f == 0 else f"xs{f}", was("fh"))
                for cc in range(CC):
                    i1 = pe.transpose(FA[:, cc * P:(cc + 1) * P], xs[:, f % 2, cc * P:(cc + 1) * P], ident)
                done("pe", f"fxt{f}", i1)
                wait(act, f"fxt{f}", was("fhm"))
                done("act", f"fx{f}", act.activation(xsT[:, :, :].rearrange("p c n -> p (c n)"), FA[:, 0:C], ACT.Copy))
                ev = pe.value_load(expert[0:1, bass.ds(first + f, 1)], min_val=0, max_val=E - 1)
                if f == FPI - 1:
                    wait(sp, f"fxt{f}")
                    done("q_xs0", "xs0", sp.dma_start(xs[:, 0, :], xs_d[bass.ds((first + FPI) * P, P), :]))
                av = act.value_load(expert[0:1, bass.ds(first + f, 1)], min_val=0, max_val=E - 1)
                yield 0.5
                wait(pe, f"fx{f}", was("fy"), "ew1")
                for cc in range(CC):
                    i1 = pe.matmul(FB[:, :], xsT[:, cc, :], w1[:, bass.ds(ev * (CC * HID) + cc * HID, HID)], start=(cc == 0), stop=(cc == 1))
                done("pe", f"fhm{f}", i1)
                yield 1.7
                wait(act, f"fhm{f}", was("fht"))
                done("act", f"fhc{f}", act.activation(hs[:, :], FB[:, :], ACT.Copy))
                yield 0.0
                wait(pe, f"fhc{f}")
                for k in range(HC):
                    i1 = pe.transpose(FA[:, k * P:(k + 1) * P], hs[:, k * P:(k + 1) * P], ident)
                done("pe", f"fht{f}", i1)
                yield 0.5
                wait(act, f"fht{f}", was("fym"))
                for k in range(HC):
                    i1 = act.activation(hsT[:, k, :], FA[:, k * P:(k + 1) * P], ACT.Relu, bias=b1c[:, bass.ds(av * HC + k, 1)])
                done("act", f"fh{f}", i1)
                yield 0.0
                wait(pe, f"fh{f}", "ew2")
                for k in range(HC):
                    i1 = pe.matmul(FB[:, 0:C], hsT[:, k, :], w2[:, bass.ds(ev * (HC * C) + k * C, C)], start=(k == 0), stop=(k == HC - 1))
                done("pe", f"fym{f}", i1)
                yield 1.7
                wait(dve, f"fym{f}", f"b2{f}", was("ys"))
                done("dve", f"fy{f}", dve.tensor_tensor(ys[:, :], FB[:, 0:C], b2t[:, f % 2, :], ALU.add))
                wait(sp, f"fy{f}")
                done("q_ys", f"ys{f}", sp.dma_start(ys_d[bass.ds(first * P + f * P, P), :], ys[:, :]))

        def chain(*parts):
            for part in parts:
                yield from part

        fl.stream = "route"
        route = routing()
        for _ in range(4):
            next(route)
        fl.stream = "setup"
        for e in (pe, dve, act, pool):
            wait(e, "ln/h0", "ln/h1", "ln/hm0", "ln/hm1", "ln/xx0", "ln/xx1", "ln/xt0", "ln/xt1",
                 "ln/lt0", "ln/lt1", "ln/lc0", "ln/lc1", "wv_c", "bst", "w")
        wait(sp, "ln/zero", "zero2", "ln/cs0", "ln/cs1")
        wait(act, "bst")
        done("pool", "z_AT0", pool.memset(aT, 0.0))
        for e in (pe, dve, act):
            wait(e, "z_S", "z_AT0")
        fl.stream = "codes"
        load = codes(0, 0)
        next(load)
        done("q_ew1", "ew1", sp.dma_start(b1c[:, :], io["b1c"]))
        for e in range(E):
            done("q_ew1", "ew1", sp.dma_start(w1[:, e * CC * HID:(e + 1) * CC * HID].rearrange("p (c n) -> p c n", c=CC),
                                              io["W1"][e].rearrange("(c p) n -> p c n", p=P)))
        for _ in load:
            pass
        wait(pe, "clo.0")

        fl.enter("pre")
        interleave("a", ("front", chain(front(0, 0), front(1, 0))), ("pairs", pairs(0, 0)), ("route", route),
                   ("codes", chain(codes(1, 0), codes(0, 1))))
        fl.leave()
        fl.stream = "setup"
        wait(sp, "pre/scat")
        fl.place, fl.stream = "pre", "experts"
        done("q_xs0", "xs0", sp.dma_start(xs[:, 0, :], xs_d[0:P, :]))
        fl.place, fl.stream = "once", "setup"
        for e in range(E):
            done("q_ew2", "ew2", sp.dma_start(w2[:, e * HC * C:(e + 1) * HC * C].rearrange("p (c n) -> p c n", c=HC),
                                              io["W2"][e].rearrange("(c p) n -> p c n", p=P)))
        wait(pool, "pre/r_ex")
        done("pool", "z_AT1", pool.memset(aT1, 0.0))
        for e in (pe, dve, act, sp):
            wait(e, "z_AT1", "pre/r_ex")
        with nc.Fori(0, TURNS) as c:
            fl.enter("main", TURNS, c)
            interleave("a", ("pairs", chain(pairs(1, c), pairs(0, c + 1))), ("tail", chain(tail(0, c), tail(1, c))),
                       ("front", chain(front(0, c + 1), front(1, c + 1))), ("experts", experts(c * FPI, FPI)),
                       ("codes", chain(codes(1, c + 1), codes(0, c + 2))))
            fl.leave()
        LASTF = FT - TURNS * FPI - 1
        adr = at_d.rearrange("(b k p) c -> b p k c", b=NB, p=P)
        odr = io["out"].rearrange("(b k p) c -> b p k c", b=NB, p=P)
        fg = w1[:, 0:NT * C].rearrange("p (b k c) -> p b k c", b=NB, c=C)
        fa = w2[:, 0:NB * TURNS * C].rearrange("p (b k c) -> p b k c", b=NB, c=C)

        def gathers():
            wait(pool, f"ys{LASTF}", f"fhm{LASTF}", "gy.1")
            for b in range(NB):
                for k in range(NCH):
                    n = b * NCH + k
                    done(f"q_fg{b}", f"fg{b}", pool.indirect_dma_start(fg[:, b, k, :], None, ys_d, bass.IndirectOffsetOnAxis(slot[:, n:n + 1], 0)))
                    if k % 4 == 3:
                        yield 0.5

        def sums():
            wait(sp, f"ys{LASTF}", f"fym{LASTF}", ("st.0", 1), ("st.1", 1))
            for b in range(NB):
                done(f"q_fa{b}", f"fa{b}", sp.dma_start(fa[:, b, :, :], adr[b, :, 0:TURNS, :]))
            yield 0.0
            for b in range(NB):
                for half in (range(0, 4), range(4, TURNS)):
                    wait(dve, f"fa{b}", f"fg{b}")
                    for k in half:
                        n = b * NCH + k
                        i1 = dve.scalar_tensor_tensor(fa[:, b, k, :], fg[:, b, k, :], prob[:, n:n + 1], fa[:, b, k, :], ALU.mult, ALU.add)
                    done("dve", f"fs{b}{half[0]}", i1)
                    yield 0.0
                wait(sp, f"fs{b}4")
                done("q_out", "out", sp.dma_start(odr[b, :, 0:TURNS, :], fa[:, b, :, :]))
                yield 0.0

        fl.enter("last")
        interleave("a", ("pairs", pairs(1, NCH - 1)), ("tail", chain(tail(0, NCH - 1), tail(1, NCH - 1))),
                   ("experts", experts(TURNS * FPI, FT - TURNS * FPI)), ("end", gathers()), ("sums", sums()))
        fl.stream = "end"
        for u in range(2):
            wait(dve, f"o.{u}", *[f"fg{UB * u + b}" for b in range(UB)])
            for b in range(UB):
                n = (UB * u + b) * NCH + NCH - 1
                i1 = dve.scalar_tensor_tensor(res[:, u, b, :], fg[:, UB * u + b, NCH - 1, :], prob[:, n:n + 1], res[:, u, b, :], ALU.mult, ALU.add)
            done("dve", f"fl{u}", i1)
            wait(sp, f"fl{u}")
            done("q_out", "out", sp.dma_start(odr[UB * u:UB * (u + 1), :, NCH - 1, :].rearrange("b p c -> p b c"), res[:, u, :, :]))
        wait(sp, "out")
        fl.leave()
        return fl.summary()


def constants():
    con = np.zeros((P, NCONST), np.float32)
    con[:, IDN:IDN + P] = np.eye(P)
    a = np.arange(P)
    rout = np.zeros((P, NROUTE), np.float32)
    con[:, TRI:TRI + P] = a[:, None] < a[None]
    con[:, ONE:ONE + P] = 1
    rout[:, RANK8:RANK8 + NT * E] = np.tile(E - np.arange(E), NT)
    rout[:, TILE_AT:TILE_AT + E * NT] = np.tile(P * np.arange(NT), E)
    rout[:, TILE_NO:] = np.repeat(np.arange(FT), E - 1)
    msk = np.zeros((P, len(LEVELS), LEAF), np.uint32)
    s, t = (a % LEAF)[:, None], np.arange(LEAF)[None]
    for n, B in enumerate(LEVELS):
        msk[:, n] = (s == t) if B == 0 else (s // (2 * B) == t // (2 * B)) & (s % (2 * B) < B) & (t % (2 * B) >= B)
    return con, rout, msk


def kernel(**inp):
    import concourse.bacc as _bacc
    from concourse.bass_utils import run_bass_kernel_spmd as _run

    g = {k.replace("L0_attn_", "a_").replace("L0_ffn_", "f_"): np.asarray(v) for k, v in inp.items()}
    con, rout, msk = constants()
    col = lambda v: v.reshape(-1, CC, P).transpose(2, 0, 1).reshape(P, -1)
    vec = np.concatenate([col(g[n]) for n in ("a_miu_x", "a_td_miu", "a_u", "a_lam")], axis=1)
    arrays = {
        "x": g["a_x"].reshape(TOK, C), "con": con, "rout": rout, "msk": msk, "vec": vec,
        "gamma": g["a_gamma"].reshape(C), "beta": g["a_beta"].reshape(C),
        "A": g["a_A"], "Bp": g["a_Bp"], "tdA": g["a_tdA"], "tdB": g["a_tdB"],
        "WkT": g["a_Wk"].T, "WvT": g["a_Wv"].T, "WrT": g["a_Wr"].T, "WoT": g["a_Wo"].T,
        "Wg1": g["a_Wg1"], "Wg2": g["a_Wg2"], "Wr": g["f_Wr"], "br": g["f_br"].reshape(E, 1),
        "W1": g["f_W1"], "W2": g["f_W2"], "b1c": g["f_b1"].reshape(E * HC, P).T, "b2": g["f_b2"].reshape(E * C),
    }
    arrays = {k: np.ascontiguousarray(v) for k, v in arrays.items()}

    known = None
    for _ in range(2):
        nc = _bacc.Bacc("TRN2", target_bir_lowering=False, num_devices=1)
        io = {k: nc.dram_tensor(f"in_{k}", v.shape, mybir.dt.from_np(v.dtype), kind="ExternalInput").ap()
              for k, v in arrays.items()}
        io["out"] = nc.dram_tensor("out", (TOK, C), F32, kind="ExternalOutput").ap()
        known = program(nc, io, known)
    r = _run(nc, [{f"in_{k}": v for k, v in arrays.items()}], core_ids=[0])
    return r.results[0]["out"].reshape(NB, T, C)
```
